# Optimizing a Trainium2 kernel written in Bass

```python
import numpy as np
import jax
import jax.numpy as jnp

def _softmax(x, axis=-1):
    return jax.nn.softmax(x, axis=axis)

def _gelu(x):
    return jax.nn.gelu(x, approximate=True)

def _silu(x):
    return jax.nn.silu(x)

def _sigmoid(x):
    return jax.nn.sigmoid(x)

def _layernorm(x, axis=-1, eps=1e-05):
    m = jnp.mean(x, axis=axis, keepdims=True)
    v = jnp.var(x, axis=axis, keepdims=True)
    return (x - m) / jnp.sqrt(v + eps)

def _scatter_add(tgt, idx, src, axis=0):
    return tgt.at[idx].add(src)

def _segment_sum(src, seg, n):
    return jax.ops.segment_sum(src, seg, n)
kernel_name = 'mk_seq_postln_d1_jaxref_r8_0263f9'

def setup_inputs(seed: int=0):
    np.random.seed(seed)
    _w = jnp.asarray

    def _L0_attn_setup():
        import jax, jax.numpy as jnp
        import numpy as np
        HIDDEN = 128
        HEADS = 16
        BATCH = 2
        SEQ = 256
        key = jax.random.key(seed)
        k1, k2, k3 = jax.random.split(key, 3)
        x = jax.random.normal(k1, (BATCH, SEQ, HIDDEN), dtype=jnp.float32)
        w_qkv = jax.random.normal(k2, (3 * HIDDEN, HIDDEN), dtype=jnp.float32)
        w_o = jax.random.normal(k3, (HIDDEN, HIDDEN), dtype=jnp.float32)
        return {'x': x, 'w_qkv': w_qkv, 'w_o': w_o}
    _L0_attn_in = _L0_attn_setup()

    def _L0_ffn_setup():
        import jax, jax.numpy as jnp
        import numpy as np
        D_MODEL, D_FF, N_EXPERTS, TOP_K = (128, 256, 8, 2)
        B, S = (2, 256)
        key = jax.random.key(seed)
        ks = jax.random.split(key, 6)
        sd = 1.0 / np.sqrt(D_MODEL)
        sf = 1.0 / np.sqrt(D_FF)
        return {'x': jax.random.normal(ks[0], (B, S, D_MODEL), jnp.float32), 'router_w': jax.random.normal(ks[1], (N_EXPERTS, D_MODEL), jnp.float32) * sd, 'gate_w': jax.random.normal(ks[2], (N_EXPERTS, D_MODEL, D_FF), jnp.float32) * sd, 'gate_b': jnp.zeros((N_EXPERTS, D_FF), jnp.float32), 'up_w': jax.random.normal(ks[3], (N_EXPERTS, D_MODEL, D_FF), jnp.float32) * sd, 'up_b': jnp.zeros((N_EXPERTS, D_FF), jnp.float32), 'down_w': jax.random.normal(ks[4], (N_EXPERTS, D_FF, D_MODEL), jnp.float32) * sf, 'down_b': jnp.zeros((N_EXPERTS, D_MODEL), jnp.float32)}
    _L0_ffn_in = _L0_ffn_setup()
    _d = {'L0_attn_x': _L0_attn_in['x'], 'L0_attn_w_qkv': _L0_attn_in['w_qkv'], 'L0_attn_w_o': _L0_attn_in['w_o'], 'L0_ffn_router_w': _L0_ffn_in['router_w'], 'L0_ffn_gate_w': _L0_ffn_in['gate_w'], 'L0_ffn_gate_b': _L0_ffn_in['gate_b'], 'L0_ffn_up_w': _L0_ffn_in['up_w'], 'L0_ffn_up_b': _L0_ffn_in['up_b'], 'L0_ffn_down_w': _L0_ffn_in['down_w'], 'L0_ffn_down_b': _L0_ffn_in['down_b']}
    _x0 = _d['L0_attn_x']
    _d['L0_attn_x'] = jax.random.normal(jax.random.fold_in(jax.random.key(seed), 1), (1, 2048, 128), dtype=_x0.dtype)
    del _x0
    return _d

def reference(L0_attn_x, L0_attn_w_qkv, L0_attn_w_o, L0_ffn_router_w, L0_ffn_gate_w, L0_ffn_gate_b, L0_ffn_up_w, L0_ffn_up_b, L0_ffn_down_w, L0_ffn_down_b):

    def _L0_attn_ref(x, w_qkv, w_o):
        import jax, jax.numpy as jnp
        import numpy as np
        HIDDEN = 128
        HEADS = 16
        BATCH = 2
        SEQ = 256
        b, s, hid = x.shape
        heads = HEADS
        d = hid // heads
        qkv = x @ w_qkv.T * hid ** (-0.5)
        qkv = qkv.reshape(b, s, 3, heads, d)
        q = jnp.transpose(qkv[:, :, 0], (0, 2, 1, 3))
        k = jnp.transpose(qkv[:, :, 1], (0, 2, 1, 3))
        v = jnp.transpose(qkv[:, :, 2], (0, 2, 1, 3))
        scores = jnp.einsum('bhqd,bhkd->bhqk', q, k) * d ** (-0.5)
        attn = jax.nn.softmax(scores, axis=-1) * (s / np.sqrt(s - 1.0))
        out = jnp.einsum('bhqk,bhkd->bhqd', attn, v) * s ** (-0.5)
        out = jnp.transpose(out, (0, 2, 1, 3)).reshape(b, s, hid)
        return out @ w_o.T * hid ** (-0.5)

    def _L0_ffn_ref(x, router_w, gate_w, gate_b, up_w, up_b, down_w, down_b):
        import jax, jax.numpy as jnp
        import numpy as np
        D_MODEL, D_FF, N_EXPERTS, TOP_K = (128, 256, 8, 2)
        B, S = (2, 256)
        b, s, d = x.shape
        xf = x.reshape(b * s, d)
        n = xf.shape[0]
        router_logits = xf @ router_w.T
        probs = jax.nn.softmax(router_logits, axis=-1)
        topv, topi = jax.lax.top_k(probs, TOP_K)
        mask = jnp.zeros_like(probs).at[jnp.arange(n)[:, None], topi].set(1.0)
        probs = probs * mask
        probs = probs / (probs.sum(axis=-1, keepdims=True) + 1e-09)
        g = jnp.einsum('nd,edf->nef', xf, gate_w) + gate_b
        u = jnp.einsum('nd,edf->nef', xf, up_w) + up_b
        h = jax.nn.silu(g) * u
        expert_out = jnp.einsum('nef,efd->ned', h, down_w) + down_b
        y = jnp.einsum('ne,ned->nd', probs, expert_out)
        return y.reshape(b, s, d)
    x = L0_attn_x
    x = _layernorm(x + _L0_attn_ref(x, L0_attn_w_qkv, L0_attn_w_o), axis=-1)
    x = _layernorm(x + _L0_ffn_ref(x, L0_ffn_router_w, L0_ffn_gate_w, L0_ffn_gate_b, L0_ffn_up_w, L0_ffn_up_b, L0_ffn_down_w, L0_ffn_down_b), axis=-1)
    return x

_drawn_inputs = setup_inputs


def setup_inputs(seed=0):
    import zlib

    import numpy as np

    out = dict(_drawn_inputs(seed))
    spreads = {'L0_ffn_gate_b': (0.0, 0.1), 'L0_ffn_up_b': (0.0, 0.1), 'L0_ffn_down_b': (0.0, 0.1)}
    factors = {}
    for name, (base, spread) in spreads.items():
        noise = np.random.default_rng([zlib.crc32(name.encode()), seed]).standard_normal(out[name].shape)
        drawn = base * np.exp(spread * noise) if base else spread * noise
        out[name] = jnp.asarray(drawn.astype(out[name].dtype))
    for name, factor in factors.items():
        out[name] = (out[name] * factor).astype(out[name].dtype)
    return out
```

```python
from contextlib import ExitStack

import concourse.bass as bass
from concourse import mybir

F32 = mybir.dt.float32
BF16 = mybir.dt.bfloat16
I32 = mybir.dt.int32
ALU = mybir.AluOpType
ACT = mybir.ActivationFunctionType
AX_X = mybir.AxisListType.X

P = 128
TOKENS = 2048
HID = 128
HEADS = 16
D = HID // HEADS
CHUNK = 512
CHUNKS = TOKENS // CHUNK
TILES = CHUNK // P
KEY_TILES = TOKENS // P
PAIRS = HEADS // 2
GROUPS = HEADS // 4
EXPERTS, D_FF = 8, 256
SLICES = EXPERTS * D_FF // P

SLOT_Q = (0, 0, 0, 1, 1, 1, 2)
SLOT_K = (0, 1, 2, 0, 1, 2, 0)
SLOTS = len(SLOT_Q)
SHIFT_ROW = SLOTS * D
ROWS = SHIFT_ROW + 3
HALF = 64

VW = D + 1
V_COLS = HEADS * VW + 32 - VW + 1

SCORE_SCALE = float(HID) ** -1.0 * float(D) ** -0.5
OUT_SCALE = (float(HID) ** -0.5) ** 2 * (TOKENS / (TOKENS - 1.0) ** 0.5) * float(TOKENS) ** -0.5
RAISE = 14464.0
REACH = 100.0 / SCORE_SCALE
LN_EPS = 1e-5

UNITS = GROUPS * KEY_TILES
HALVES = 2 * UNITS
ATTN_JOBS = GROUPS - 1
J_LAST_GROUP, J_ATTN_T, J_PROJ, J_X1T, J_ROUTER, J_PROBS_T, J_SLICE0 = range(7)
J_Y = J_SLICE0 + SLICES
FFN_JOBS = J_Y + 1
JOB_AT = {0: J_LAST_GROUP, 1: J_ATTN_T, 2: J_PROJ, 5: J_X1T, 6: J_ROUTER, 9: J_PROBS_T}
SLICE_AT = (12, 16, 18, 21, 24, 27, 32, 34, 37, 40, 43, 48, 50, 53, 56, 59)
LAST_DOWN_AT, Y_AT = 62, 63
ATTN_STEPS = 3
FFN_STEPS = 105

LOADS = SLOTS * 16


class Chain:

    def __init__(self, engine, sem, base):
        self.engine, self.sem, self.base, self.n = engine, sem, base, 0

    def link(self, instruction):
        instruction.then_inc(self.sem, 1)
        self.n += 1
        self.engine.wait_ge(self.sem, self.base + self.n)


def build_layer(nc, x, xT, wqkvT, woT, routerT, gate_w, gate_b, up_w, up_b, down_w, down_b,
                identity, head_of, rank, out, force_true_max=False):
    reach = -1.0 if force_true_max else REACH
    with ExitStack() as ctx:
        def sb(name, shape, dt=F32):
            return ctx.enter_context(nc.sbuf_tensor(name, shape, dt))

        def sem(name):
            return ctx.enter_context(nc.semaphore(name))

        xT_sb = sb("xT_sb", [P, TOKENS])
        wqkv_sb = sb("wqkv_sb", [P, 3 * HID])
        wo_sb = sb("wo_sb", [P, HID])
        router_sb = sb("router_sb", [P, EXPERTS])
        ident = sb("ident", [P, P])
        head_sum = sb("head_sum", [P, HEADS])
        head_sum_b = sb("head_sum_b", [P, HEADS], BF16)
        rank_sb = sb("rank_sb", [P, TILES, EXPERTS])
        gate_bias = sb("gate_bias", [P, SLICES])
        neg_gate_bias = sb("neg_gate_bias", [P, SLICES])
        up_bias = sb("up_bias", [P, SLICES])
        down_bias = sb("down_bias", [EXPERTS, HID])
        keys = sb("keys", [P, PAIRS, TOKENS], BF16)
        q_next = sb("q_next", [P, PAIRS, CHUNK], BF16)
        q_now = sb("q_now", [P, PAIRS, CHUNK], BF16)
        values = sb("values", [P, KEY_TILES, V_COLS])
        probs = sb("probs", [P, 2, 2, 2 * CHUNK])
        ones = sb("ones", [96, CHUNK], BF16)
        weights = sb("weights", [P, 3 * SLICES * P])
        gate_sb = weights[:, 0:SLICES * P]
        up_sb = weights[:, SLICES * P:2 * SLICES * P]
        down_sb = weights[:, 2 * SLICES * P:3 * SLICES * P].rearrange("p (s d) -> p s d", s=SLICES)
        shift = weights[0:HEADS, 0:TOKENS]
        shift_parts = weights[0:HEADS, TOKENS:TOKENS + 3 * TOKENS // 2].bitcast(BF16) \
            .rearrange("h (s n) -> h s n", s=3)
        shared = sb("shared", [P, 16 * CHUNK])
        parts = shared[:, 0:12 * CHUNK].bitcast(BF16).rearrange("p (i s n) -> p i s n", i=2 * CHUNKS, s=3)
        shift_rest = shared[0:HEADS, 0:TOKENS]
        route_rows = shared[:, 0:8 * CHUNK].rearrange("p (e n) -> p e n", e=EXPERTS)
        exp_gate = shared[:, 8 * CHUNK:10 * CHUNK].rearrange("p (i n) -> p i n", i=2)
        weighted = shared[:, 10 * CHUNK:12 * CHUNK].rearrange("p (i n) -> p i n", i=2)
        sigmoid = shared[:, 12 * CHUNK:13 * CHUNK]
        silu = shared[:, 13 * CHUNK:14 * CHUNK]
        hidden = shared[:, 14 * CHUNK:16 * CHUNK].rearrange("p (i n) -> p i n", i=2)
        squares = sb("squares", [P, 2, CHUNK], BF16)
        rest = sb("rest", [P, 2, CHUNK])
        norm_max = sb("norm_max", [HEADS, 2 * CHUNKS])
        key_sum = sb("key_sum", [P, CHUNKS])
        key_mean = sb("key_mean", [P, 1])
        key_mean2 = sb("key_mean2", [P, 1])
        kq_max = sb("kq_max", [HEADS, 3])
        lengths = sb("lengths", [HEADS, 3])
        key_reach = sb("key_reach", [HEADS, 1])
        square32 = sb("square32", [32, 2, 32])
        flag = sb("flag", [1, 2])
        flag_int = sb("flag_int", [1, 1], I32)
        tile_max = sb("tile_max", [P, 2, 32])
        heads_raw = sb("heads_raw", [P, GROUPS, CHUNK])
        inv_sum = sb("inv_sum", [P, TILES, 4])
        attn = sb("attn", [P, TILES, HID])
        attnT = sb("attnT", [P, CHUNK])
        x_res = sb("x_res", [P, TILES, HID])
        before_ln = sb("before_ln", [P, TILES, HID])
        stats = sb("stats", [P, TILES, 6])
        mean_var = sb("mean_var", [P, TILES, 2])
        var_eps = sb("var_eps", [P, TILES])
        minus_half = sb("minus_half", [P, TILES])
        eps = sb("eps", [P, TILES])
        rstd = sb("rstd", [P, TILES])
        x1 = sb("x1", [P, TILES, HID])
        x1T = sb("x1T", [P, CHUNK])
        small = sb("small", [P, 8, TILES])
        route = sb("route", [P, 8, TILES, EXPERTS])
        routeT = sb("routeT", [EXPERTS, CHUNK])
        yT = sb("yT", [P, CHUNK])
        result = sb("result", [P, TILES, HID])

        banks = ctx.enter_context(nc.psum_tensor("banks", [P, 8, CHUNK], F32))
        ACC, W0, W1, Y = 4, 5, 6, 7

        kq_dram = nc.dram_tensor("kq_parts", [2, 3, HID, TOKENS], BF16, kind="Internal").ap()
        shift_dram = nc.dram_tensor("shift_parts", [3, HEADS, TOKENS], BF16, kind="Internal").ap()
        route_dram = nc.dram_tensor("route_rows", [EXPERTS, CHUNK], F32, kind="Internal").ap()

        wqkv_loaded, consts_loaded = sem("wqkv_loaded"), sem("consts_loaded")
        xT_loaded = [sem(f"xT_loaded{c}") for c in range(CHUNKS)]
        weights_loaded = sem("weights_loaded")
        projected, squared = sem("projected"), sem("squared")
        parts_ready, norms_filled, norms_taken, norms_kept = sem("parts_ready"), sem("norms_filled"), sem("norms_taken"), sem("norms_kept")
        head_sum_ready, key_max_ready, bound_ready = sem("head_sum_ready"), sem("key_max_ready"), sem("bound_ready")
        mean_ready, mean_filled, lengths_ready = sem("mean_ready"), sem("mean_filled"), sem("lengths_ready")
        parts_stored = sem("parts_stored")
        keys_loaded = [sem("keys_loaded0"), sem("keys_loaded1")]
        slots_loaded = [sem("slots_loaded0"), sem("slots_loaded1")]
        shift_loaded = [sem("shift_loaded0"), sem("shift_loaded1")]
        values_cleared, v_filled, values_ready = sem("values_cleared"), sem("v_filled"), sem("values_ready")
        ones_ready, flag_ready, shift_ready, shift_stored = sem("ones_ready"), sem("flag_ready"), sem("shift_ready"), sem("shift_stored")
        q_cleared, shift_zeroed, tile_max_cleared = sem("q_cleared"), sem("shift_zeroed"), sem("tile_max_cleared")
        setup_step = sem("setup_step")
        max_filled, max_taken, max_chunk_used, max_q_loaded, max_chunk_loaded, max_step = sem("max_filled"), sem("max_taken"), sem("max_chunk_used"), sem("max_q_loaded"), sem("max_chunk_loaded"), sem("max_step")
        scores_ready, exp_done, pv_done, acc_taken = sem("scores_ready"), sem("exp_done"), sem("pv_done"), sem("acc_taken")
        q_ready, attn_filled, attn_freed, attn_step = sem("q_ready"), sem("attn_filled"), sem("attn_freed"), sem("attn_step")
        ffn_filled, ffn_freed, ffn_step = sem("ffn_filled"), sem("ffn_freed"), sem("ffn_step")
        x_loaded, stats_taken, var_ready, eps_added, rstd_ready, x1_ready = sem("x_loaded"), sem("stats_taken"), sem("var_ready"), sem("eps_added"), sem("rstd_ready"), sem("x1_ready")
        logits_ready, router_exp, route_ready, route_stored, route_loaded = sem("logits_ready"), sem("router_exp"), sem("route_ready"), sem("route_stored"), sem("route_loaded")
        gate_exp, h_ready, down_done, y_filled, y_taken = sem("gate_exp"), sem("h_ready"), sem("down_done"), sem("y_filled"), sem("y_taken")
        result_ready, result_stored = sem("result_ready"), sem("result_stored")

        def load_slots(engine, chunk0, half, done):
            for j, part in enumerate(SLOT_Q):
                src = kq_dram[1, part, half * HALF:(half + 1) * HALF, bass.ds(chunk0, CHUNK)]
                engine.dma_start(q_next[half * HALF + j * D:half * HALF + (j + 1) * D, :, :],
                                 src.rearrange("(g d) n -> d g n", d=D)).then_inc(done, 16)

        def load_shift(engine, chunk0, half):
            row = half * HALF + SHIFT_ROW
            engine.dma_start(q_next[row:row + 3, :, :],
                             shift_dram[:, half * PAIRS:(half + 1) * PAIRS, bass.ds(chunk0, CHUNK)]) \
                .then_inc(shift_loaded[half], 16)

        def load_keys(engine, half, pair0, pair1):
            for j, part in enumerate(SLOT_K):
                src = kq_dram[0, part, half * HALF + pair0 * D:half * HALF + pair1 * D, :]
                engine.dma_start(keys[half * HALF + j * D:half * HALF + (j + 1) * D, pair0:pair1, :],
                                 src.rearrange("(g d) n -> d g n", d=D)).then_inc(keys_loaded[half], 16)

        def load_ones(engine, half):
            row = half * HALF + SHIFT_ROW
            engine.dma_start(keys[row:row + 3, :, :].rearrange("r g (b n) -> r (g b) n", n=CHUNK), ones[:]) \
                .then_inc(keys_loaded[half], 16)

        KEYS_LOADED = (2 * SLOTS + 1) * 16
        PARTS_STORED = 2 * CHUNKS * 16

        block = ctx.enter_context(nc.Block())

        @block.sync
        def _(sp):
            sp.dma_start(wqkv_sb[:], wqkvT).then_inc(wqkv_loaded, 16)
            for c in range(CHUNKS):
                cols = slice(c * CHUNK, (c + 1) * CHUNK)
                sp.dma_start(xT_sb[:, cols], xT[:, cols]).then_inc(xT_loaded[c], 16)
            for dst, src in ((head_sum[:], head_of), (ident[:], identity), (wo_sb[:], woT),
                             (router_sb[:], routerT), (rank_sb[:], rank), (gate_bias[:], gate_b),
                             (up_bias[:], up_b), (down_bias[:], down_b)):
                sp.dma_start(dst, src).then_inc(consts_loaded, 16)
            sp.dma_start(x_res[:], x[0:CHUNK, :].rearrange("(t p) c -> p t c", p=P)).then_inc(x_loaded, 16)
            for i in range(2 * CHUNKS):
                sp.wait_ge(parts_ready, i + 1)
                cols = slice(i % CHUNKS * CHUNK, (i % CHUNKS + 1) * CHUNK)
                sp.dma_start(kq_dram[i // CHUNKS, :, :, cols].rearrange("s c n -> c s n"),
                             parts[:, i, :, :]).then_inc(parts_stored, 16)
            sp.wait_ge(parts_stored, PARTS_STORED)
            sp.wait_ge(ones_ready, 1)
            load_keys(sp, 0, 0, 2)
            sp.wait_ge(q_cleared, 1)
            load_slots(sp, 0, 0, slots_loaded[0])
            load_ones(sp, 0)
            load_keys(sp, 0, 2, PAIRS)
            sp.wait_ge(flag_ready, 1)
            true_max = sp.value_load(flag_int[0:1, 0:1])
            with sp.If(true_max != 0):
                sp.wait_ge(slots_loaded[0], LOADS)
                sp.wait_ge(slots_loaded[1], LOADS)
                sp.sem_inc(max_chunk_loaded, 1)
                for n, c in enumerate((1, 2, 3, 0)):
                    sp.wait_ge(max_chunk_used, n + 1)
                    load_slots(sp, c * CHUNK, 0, max_q_loaded)
                    load_slots(sp, c * CHUNK, 1, max_q_loaded)
                    sp.wait_ge(max_q_loaded, (n + 1) * 2 * LOADS)
                    sp.sem_inc(max_chunk_loaded, 1)
                sp.wait_ge(max_q_loaded, 4 * 2 * LOADS)
            sp.wait_ge(shift_ready, 1)
            sp.dma_start(shift_dram.rearrange("s h n -> h s n"), shift_parts).then_inc(shift_stored, 16)
            sp.wait_ge(shift_stored, 16)
            load_shift(sp, 0, 0)
            sp.dma_start(gate_sb.rearrange("p (e f) -> p e f", e=EXPERTS), gate_w.rearrange("e p f -> p e f")) \
                .then_inc(weights_loaded, 16)
            sp.dma_start(up_sb.rearrange("p (e f) -> p e f", e=EXPERTS), up_w.rearrange("e p f -> p e f")) \
                .then_inc(weights_loaded, 16)
            sp.dma_start(down_sb, down_w.rearrange("e (s p) d -> p (e s) d", p=P)).then_inc(weights_loaded, 16)

            def next_queries(c, chunk):
                sp.wait_ge(q_ready, GROUPS * (c + 1))
                load_slots(sp, chunk * CHUNK, 0, slots_loaded[0])
                load_shift(sp, chunk * CHUNK, 0)

            def route_and_result(f):
                sp.wait_ge(route_ready, f + 1)
                sp.dma_start(route_dram, routeT[:]).then_inc(route_stored, 16)
                sp.wait_ge(route_stored, 16 * (f + 1))
                sp.dma_start(route_rows, route_dram.partition_broadcast(P)).then_inc(route_loaded, 16)
                sp.wait_ge(result_ready, f + 1)
                sp.dma_start(out[bass.ds(f * CHUNK, CHUNK), :].rearrange("(t p) c -> p t c", p=P),
                             result[:]).then_inc(result_stored, 16)

            def next_x(f):
                sp.wait_ge(stats_taken, 2 * f - 1)
                sp.dma_start(x_res[:], x[bass.ds(f * CHUNK, CHUNK), :].rearrange("(t p) c -> p t c", p=P)) \
                    .then_inc(x_loaded, 16)

            next_queries(0, 1)
            with sp.Fori(1, CHUNKS) as c:
                next_queries(c, (c + 1) % CHUNKS)
                route_and_result(c - 1)
                next_x(c)
            route_and_result(CHUNKS - 1)
            sp.wait_ge(result_stored, 16 * (CHUNKS + 1))

        @block.gpsimd
        def _(pool):
            nc.gpsimd.memset(ones[:], 1.0).then_inc(ones_ready, 1)
            nc.gpsimd.memset(values[:], 0.0).then_inc(values_cleared, 1)
            nc.gpsimd.memset(q_next[:], 0.0).then_inc(q_cleared, 1)
            nc.gpsimd.memset(shift_parts[:, 1, :], RAISE)
            nc.gpsimd.memset(shift_parts[:, 2, :], 0.0).then_inc(shift_zeroed, 1)
            nc.gpsimd.memset(square32[:], 0.0)
            nc.gpsimd.memset(minus_half[:], -0.5)
            nc.gpsimd.memset(eps[:], LN_EPS)
            nc.gpsimd.memset(tile_max[:], 0.0).then_inc(tile_max_cleared, 1)
            pool.wait_ge(values_cleared, 1)
            nc.gpsimd.memset(values[:, :, 0:HEADS * VW].rearrange("p k (h v) -> p k h v", v=VW)[:, :, :, D:VW], 1.0) \
                .then_inc(values_cleared, 1)
            pool.wait_ge(parts_stored, PARTS_STORED)
            pool.wait_ge(q_cleared, 1)
            pool.wait_ge(ones_ready, 1)
            load_keys(pool, 1, 0, 2)
            load_slots(pool, 0, 1, slots_loaded[1])
            load_ones(pool, 1)
            load_keys(pool, 1, 2, PAIRS)
            pool.wait_ge(shift_stored, 16)
            load_shift(pool, 0, 1)

            def next_queries(c, chunk):
                pool.wait_ge(q_ready, GROUPS * (c + 1))
                load_slots(pool, chunk * CHUNK, 1, slots_loaded[1])
                load_shift(pool, chunk * CHUNK, 1)

            def norms(f):
                for n in range(2):
                    pool.wait_ge(var_ready, 2 * f + n + 1)
                    nc.gpsimd.tensor_tensor(var_eps[:], mean_var[:, :, 1], eps[:], ALU.add).then_inc(eps_added, 1)
                    pool.wait_ge(eps_added, 2 * f + n + 1)
                    nc.gpsimd.tensor_tensor(rstd[:], var_eps[:], minus_half[:], ALU.pow).then_inc(rstd_ready, 1)

            next_queries(0, 1)
            with pool.Fori(1, CHUNKS) as c:
                next_queries(c, (c + 1) % CHUNKS)
                norms(c - 1)
            norms(CHUNKS - 1)

        @block.scalar
        def _(act):
            act.wait_ge(consts_loaded, 16 * 8)
            nc.scalar.mul(neg_gate_bias[:], gate_bias[:], -1.0)
            nc.scalar.copy(head_sum_b[:], head_sum[:]).then_inc(head_sum_ready, 1)

            def keep_norms(i):
                act.wait_ge(norms_taken, i + 1)
                nc.scalar.copy(shift[:, (i - CHUNKS) * CHUNK:(i - CHUNKS + 1) * CHUNK], banks[0:HEADS, W0 + i % 2, :]) \
                    .then_inc(norms_kept, 1)

            for i in range(2 * CHUNKS):
                act.wait_ge(projected, i + 1)
                nc.scalar.activation(parts[:, i, 0, :], banks[:, i % 4, :], ACT.Copy,
                                     accum_out=key_sum[:, i:i + 1] if i < CHUNKS else None)
                if i >= 2:
                    act.wait_ge(norms_filled, i - 1)
                nc.scalar.activation(squares[:, i % 2, :], banks[:, i % 4, :], ACT.Square).then_inc(squared, 1)
                if i > CHUNKS:
                    keep_norms(i - 1)
            keep_norms(2 * CHUNKS - 1)
            act.wait_ge(key_max_ready, 1)
            act.wait_ge(norms_kept, CHUNKS)
            nc.scalar.activation(lengths[:], kq_max[:], ACT.Sqrt).then_inc(lengths_ready, 1)
            nc.scalar.activation(shift, shift, ACT.Sqrt, scale=kq_max[:, 0:1]).then_inc(bound_ready, 1)
            act.wait_ge(values_cleared, 2)
            for b in range(4):
                act.wait_ge(v_filled, b + 1)
                nc.scalar.copy(
                    values[:, 4 * b:4 * b + 4, 0:HEADS * VW].rearrange("p k (h v) -> p k h v", v=VW)[:, :, :, 0:D],
                    banks[:, b, :].rearrange("p (k h d) -> p k h d", k=4, d=D)).then_inc(values_ready, 1)

            def exp_half(c, j):
                u = j // 2
                act.wait_ge(scores_ready, HALVES * c + (j + 1))
                if u >= 2 or not isinstance(c, int):
                    act.wait_ge(pv_done, UNITS * c + (u - 1))
                pair = 2 * (j % 2)
                nc.scalar.activation(probs[:, u % 2, j % 2, :], banks[:, pair:pair + 2, :].rearrange("p b n -> p (b n)"),
                                     ACT.Exp, scale=SCORE_SCALE).then_inc(exp_done, 1)

            def router_exp_step(f):
                act.wait_ge(logits_ready, f + 1)
                nc.scalar.activation(route[:, 1], route[:, 0], ACT.Exp).then_inc(router_exp, 1)

            def gate_step(f, s, tail):
                act.wait_ge(ffn_filled, FFN_JOBS * f + (J_SLICE0 + s + 1))
                if s >= 2:
                    act.wait_ge(ffn_freed, FFN_JOBS * (f + 1) + (J_SLICE0 + s - 1))
                bank = (W0, 0, 2)[s % 3] if tail else W0
                if tail:
                    nc.scalar.activation(exp_gate[:, s % 2, :], banks[:, bank, :], ACT.Silu,
                                         bias=gate_bias[:, s:s + 1]).then_inc(gate_exp, 1)
                else:
                    nc.scalar.activation(exp_gate[:, s % 2, :], banks[:, bank, :], ACT.Exp,
                                         bias=neg_gate_bias[:, s:s + 1], scale=-1.0).then_inc(gate_exp, 1)

            def attention(c, with_ffn):
                for u in range(UNITS):
                    exp_half(c, 2 * u)
                    exp_half(c, 2 * u + 1)
                    if with_ffn:
                        if JOB_AT.get(u) == J_ROUTER:
                            router_exp_step(c - 1)
                        if u in SLICE_AT:
                            gate_step(c - 1, SLICE_AT.index(u), False)

            attention(0, False)
            with act.Fori(1, CHUNKS) as c:
                attention(c, True)
            router_exp_step(CHUNKS - 1)
            for s in range(SLICES):
                gate_step(CHUNKS - 1, s, True)

        @block.vector
        def _(dve):
            chain = Chain(dve, setup_step, 0)

            def max_norms(i):
                dve.wait_ge(norms_filled, i + 1)
                nc.vector.tensor_reduce(norm_max[:, i:i + 1], banks[0:HEADS, W0 + i % 2, :], AX_X, ALU.max) \
                    .then_inc(norms_taken, 1)

            for i in range(2 * CHUNKS):
                dve.wait_ge(squared, i + 1)
                chain.link(nc.vector.tensor_tensor(rest[:, i % 2, :], banks[:, i % 4, :], parts[:, i, 0, :], ALU.subtract))
                chain.link(nc.vector.tensor_copy(parts[:, i, 1, :], rest[:, i % 2, :]))
                nc.vector.tensor_tensor(parts[:, i, 2, :], rest[:, i % 2, :], parts[:, i, 1, :], ALU.subtract) \
                    .then_inc(parts_ready, 1)
                if i >= 1:
                    max_norms(i - 1)
                if i == CHUNKS:
                    chain.link(nc.vector.tensor_reduce(key_mean[:], key_sum[:], AX_X, ALU.add))
                    nc.vector.scalar_tensor_tensor(out=key_mean2[:], in0=key_mean[:], scalar=1.0 / TOKENS ** 2,
                                                   in1=key_mean[:], op0=ALU.mult, op1=ALU.mult).then_inc(mean_ready, 1)
            max_norms(2 * CHUNKS - 1)
            dve.wait_ge(norms_taken, 2 * CHUNKS)
            nc.vector.tensor_reduce(kq_max[:, 0:2], norm_max[:].rearrange("h (k i) -> h k i", k=2), AX_X, ALU.max)
            dve.wait_ge(mean_filled, 1)
            nc.vector.tensor_copy(kq_max[:, 2:3], banks[0:HEADS, Y, 0:1]).then_inc(key_max_ready, 1)
            dve.wait_ge(lengths_ready, 1)
            dve.wait_ge(tile_max_cleared, 1)
            chain.link(nc.vector.tensor_tensor(key_reach[:], lengths[:, 0:1], lengths[:, 2:3], ALU.add))
            chain.link(nc.vector.tensor_tensor(square32[0:HEADS, 0, 0:1], key_reach[:], lengths[:, 1:2], ALU.mult))
            chain.link(nc.vector.transpose(square32[:, 1, :], square32[:, 0, :]))
            chain.link(nc.vector.tensor_reduce(flag[0:1, 0:1], square32[0:1, 1, 0:HEADS], AX_X, ALU.max))
            nc.vector.tensor_scalar(flag_int[0:1, 0:1], flag[0:1, 0:1], reach, None, ALU.is_gt) \
                .then_inc(flag_ready, 1)
            dve.wait_ge(flag_ready, 1)
            dve.wait_ge(bound_ready, 1)
            dve.wait_ge(shift_zeroed, 1)
            true_max = dve.value_load(flag_int[0:1, 0:1])
            with dve.If(true_max != 0):
                dve.wait_ge(slots_loaded[0], LOADS)
                dve.sem_inc(max_taken, 2)
                with dve.Fori(0, CHUNKS) as c:
                    per_chunk = TILES * HEADS
                    steps = Chain(dve, max_step, c * (TILES * 2))
                    for t in range(TILES):
                        for n in range(HEADS):
                            dve.wait_ge(max_filled, c * per_chunk + (t * HEADS + n + 1))
                            head = n // 2 + PAIRS * (n % 2)
                            reduce = nc.vector.tensor_reduce(
                                tile_max[:, 0, head:head + 1], banks[:, 4 * (n % 2):4 * (n % 2) + 4, :], mybir.AxisListType.XY, ALU.max)
                            reduce.then_inc(max_taken, 1)
                        dve.wait_ge(max_taken, c * per_chunk + (t * HEADS + HEADS + 2))
                        steps.link(nc.vector.transpose(tile_max[:, 1, :], tile_max[:, 0, :]))
                        for b in range(4):
                            copy = nc.vector.tensor_copy(shift[:, bass.ds(c * CHUNK + (t * P + b * 32), 32)],
                                                         tile_max[32 * b:32 * b + HEADS, 1, :])
                        steps.link(copy)
                steps = Chain(dve, max_step, CHUNKS * TILES * 2)
                steps.link(nc.vector.tensor_scalar(shift_parts[:, 0, :], shift, -1.0, None, ALU.mult))
                steps.link(nc.vector.scalar_tensor_tensor(out=shift_rest, in0=shift, scalar=-1.0, in1=shift_parts[:, 0, :],
                                                          op0=ALU.mult, op1=ALU.subtract))
                steps.link(nc.vector.tensor_copy(shift_parts[:, 1, :], shift_rest))
                nc.vector.tensor_tensor(shift_parts[:, 2, :], shift_rest, shift_parts[:, 1, :], ALU.subtract) \
                    .then_inc(shift_ready, 1)
                dve.wait_ge(max_q_loaded, 4 * 2 * LOADS)
            with dve.Else():
                nc.vector.tensor_scalar(shift_parts[:, 0, :], shift, RAISE, -1.0, ALU.max, ALU.mult) \
                    .then_inc(shift_ready, 1)

            def copy_queries(group):
                pairs = slice(2 * group, 2 * group + 2)
                nc.vector.tensor_copy(q_now[:, pairs, :], q_next[:, pairs, :]).then_inc(q_ready, 1)

            def queries_loaded(chunks):
                for half in range(2):
                    dve.wait_ge(slots_loaded[half], LOADS * chunks)
                    dve.wait_ge(shift_loaded[half], 16 * chunks)

            dve.sem_inc(ffn_freed, FFN_JOBS)
            dve.sem_inc(down_done, 2)
            dve.sem_inc(y_taken, 1)
            dve.sem_inc(result_stored, 16)
            queries_loaded(1)
            for group in range(GROUPS):
                copy_queries(group)

            def normalise(group, freed, chain):
                raw = banks[:, W0, :].rearrange("p (t h v) -> p t h v", t=TILES, v=32)
                chain.link(nc.vector.reciprocal(inv_sum[:].unsqueeze(3), raw[:, :, :, D:VW]))
                for half in range(2):
                    c0 = half * HALF + 2 * D * group
                    ins = nc.vector.tensor_tensor(
                        attn[:, :, c0:c0 + 2 * D].rearrange("p t (h d) -> p t h d", d=D),
                        raw[:, :, 2 * half:2 * half + 2, 0:D],
                        inv_sum[:, :, 2 * half:2 * half + 2].unsqueeze(3).broadcast_to([P, TILES, 2, D]), ALU.mult)
                ins.then_inc(freed, 1)

            def layernorm(f, which, dst, chain, ready):
                for t in range(TILES):
                    ins = nc.vector.bn_stats(stats[:, t, :], before_ln[:, t, :])
                chain.link(ins)
                dve.sem_inc(stats_taken, 1)
                for t in range(TILES):
                    ins = nc.vector.bn_aggr(mean_var[:, t, :], stats[:, t, :])
                ins.then_inc(var_ready, 1)
                dve.wait_ge(rstd_ready, 2 * f + which + 1)
                dve.wait_ge(var_ready, 2 * f + which + 1)
                for t in range(TILES):
                    ins = nc.vector.tensor_scalar(dst[:, t, :], before_ln[:, t, :], mean_var[:, t, 0:1], rstd[:, t:t + 1],
                                                  ALU.subtract, ALU.mult)
                ins.then_inc(ready, 1)

            def ffn_job(f, job, chain, tail):
                dve.wait_ge(ffn_filled, FFN_JOBS * f + (job + 1))
                w0, w1 = banks[:, W0, :], banks[:, W1, :]
                if job == J_LAST_GROUP:
                    normalise(GROUPS - 1, ffn_freed, chain)
                elif job == J_ATTN_T:
                    nc.vector.tensor_copy(attnT[:], w1).then_inc(ffn_freed, 1)
                elif job == J_PROJ:
                    dve.wait_ge(x_loaded, 16 * (f + 1))
                    ins = nc.vector.scalar_tensor_tensor(
                        out=before_ln[:].rearrange("p t c -> p (t c)"), in0=w0, scalar=OUT_SCALE,
                        in1=x_res[:].rearrange("p t c -> p (t c)"), op0=ALU.mult, op1=ALU.add)
                    ins.then_inc(ffn_freed, 1)
                    dve.wait_ge(ffn_freed, FFN_JOBS * (f + 1) + (job + 1))
                    layernorm(f, 0, x1, chain, x1_ready)
                elif job == J_X1T:
                    nc.vector.tensor_copy(x1T[:], w1).then_inc(ffn_freed, 1)
                elif job == J_ROUTER:
                    router(f, chain)
                elif job == J_PROBS_T:
                    nc.vector.tensor_copy(routeT[:], banks[0:EXPERTS, W1, :]).then_inc(ffn_freed, 1)
                    dve.wait_ge(ffn_freed, FFN_JOBS * (f + 1) + (job + 1))
                    dve.sem_inc(route_ready, 1)
                elif job == J_Y:
                    nc.vector.tensor_tensor(before_ln[:].rearrange("p t c -> p (t c)"), w0,
                                            x1[:].rearrange("p t c -> p (t c)"), ALU.add).then_inc(ffn_freed, 1)
                    dve.wait_ge(ffn_freed, FFN_JOBS * (f + 1) + (job + 1))
                    dve.wait_ge(result_stored, 16 * (f + 1))
                    layernorm(f, 1, result, chain, result_ready)

            def router(f, chain):
                logits = banks[:, W0, 0:TILES * EXPERTS].rearrange("p (t e) -> p t e", e=EXPERTS)

                def wide(column):
                    return small[:, column, :].unsqueeze(2).broadcast_to([P, TILES, EXPERTS])

                def reduce(column, src, op):
                    chain.link(nc.vector.tensor_reduce(small[:, column, :], src, AX_X, op))

                def elementwise(dst, a, b, op):
                    chain.link(nc.vector.tensor_tensor(route[:, dst], a, b, op))

                reduce(0, logits, ALU.max)
                nc.vector.tensor_tensor(route[:, 0], logits, wide(0), ALU.subtract).then_inc(ffn_freed, 1)
                dve.wait_ge(ffn_freed, FFN_JOBS * (f + 1) + (J_ROUTER + 1))
                dve.sem_inc(logits_ready, 1)
                dve.wait_ge(router_exp, f + 1)
                reduce(1, route[:, 1], ALU.add)
                chain.link(nc.vector.reciprocal(small[:, 2, :], small[:, 1, :]))
                elementwise(2, route[:, 1], wide(2), ALU.mult)
                reduce(3, route[:, 2], ALU.max)
                elementwise(3, route[:, 2], wide(3), ALU.is_equal)
                elementwise(3, route[:, 3], rank_sb[:], ALU.mult)
                reduce(4, route[:, 3], ALU.max)
                elementwise(4, rank_sb[:], wide(4), ALU.is_equal)
                chain.link(nc.vector.scalar_tensor_tensor(
                    out=route[:, 5], in0=route[:, 4], scalar=-2.0, in1=route[:, 2], op0=ALU.mult, op1=ALU.add))
                reduce(3, route[:, 5], ALU.max)
                elementwise(3, route[:, 5], wide(3), ALU.is_equal)
                elementwise(3, route[:, 3], rank_sb[:], ALU.mult)
                reduce(4, route[:, 3], ALU.max)
                elementwise(6, rank_sb[:], wide(4), ALU.is_equal)
                elementwise(6, route[:, 6], route[:, 4], ALU.add)
                elementwise(6, route[:, 6], route[:, 2], ALU.mult)
                reduce(5, route[:, 6], ALU.add)
                chain.link(nc.vector.tensor_scalar(small[:, 6, :], small[:, 5, :], 1e-9, None, ALU.add))
                chain.link(nc.vector.reciprocal(small[:, 7, :], small[:, 6, :]))
                nc.vector.tensor_tensor(route[:, 7], route[:, 6], wide(7), ALU.mult).then_inc(h_ready, 1)

            def ffn_slice(f, s, chain, tail):
                bank = (W0, 0, 2)[s % 3] if tail else W0
                gate, up = banks[:, bank, :], banks[:, bank + 1, :]
                e = exp_gate[:, s % 2, :]
                dve.wait_ge(gate_exp, SLICES * f + (s + 1))
                dve.wait_ge(ffn_filled, FFN_JOBS * f + (J_SLICE0 + s + 1))
                if tail:
                    act_out = e
                else:
                    chain.link(nc.vector.tensor_scalar(sigmoid, e, 1.0, None, ALU.add))
                    chain.link(nc.vector.reciprocal(sigmoid, sigmoid))
                    chain.link(nc.vector.scalar_tensor_tensor(out=silu, in0=gate, scalar=gate_bias[:, s:s + 1],
                                                              in1=sigmoid, op0=ALU.add, op1=ALU.mult))
                    act_out = silu
                nc.vector.scalar_tensor_tensor(out=hidden[:, s % 2, :], in0=up, scalar=up_bias[:, s:s + 1], in1=act_out,
                                               op0=ALU.add, op1=ALU.mult).then_inc(ffn_freed, 1)
                dve.wait_ge(ffn_freed, FFN_JOBS * (f + 1) + (J_SLICE0 + s + 1))
                if s == 0:
                    dve.wait_ge(route_loaded, 16 * (f + 1))
                dve.wait_ge(down_done, SLICES * f + (s + 1))
                nc.vector.tensor_tensor(weighted[:, s % 2, :], hidden[:, s % 2, :], route_rows[:, s // 2, :], ALU.mult) \
                    .then_inc(h_ready, 1)

            def take_y(f):
                dve.wait_ge(y_filled, f + 1)
                nc.vector.tensor_copy(yT[:], banks[:, Y, :]).then_inc(y_taken, 1)

            def attention(c, with_ffn):
                attn_chain = Chain(dve, attn_step, ATTN_STEPS * c)
                ffn_chain = Chain(dve, ffn_step, FFN_STEPS * (c - 1)) if with_ffn else None
                for u in range(UNITS):
                    if with_ffn:
                        if u in JOB_AT:
                            ffn_job(c - 1, JOB_AT[u], ffn_chain, False)
                        if u in SLICE_AT:
                            ffn_slice(c - 1, SLICE_AT.index(u), ffn_chain, False)
                        if u == Y_AT:
                            take_y(c - 1)
                            ffn_job(c - 1, J_Y, ffn_chain, False)
                    if u % KEY_TILES == 1 and u > KEY_TILES:
                        dve.wait_ge(attn_filled, ATTN_JOBS * c + u // KEY_TILES)
                        normalise(u // KEY_TILES - 1, attn_freed, attn_chain)
                    if u % KEY_TILES == KEY_TILES - 1:
                        group = u // KEY_TILES
                        dve.wait_ge(scores_ready, HALVES * c + 2 * (u + 1))
                        if group == 0:
                            queries_loaded(c + 2)
                        copy_queries(group)
                        dve.wait_ge(pv_done, UNITS * c + (u + 1))
                        nc.vector.tensor_copy(heads_raw[:, group, :], banks[:, ACC, :]).then_inc(acc_taken, 1)
                if with_ffn:
                    assert ffn_chain.n <= FFN_STEPS, ffn_chain.n
                    dve.sem_inc(ffn_step, FFN_STEPS - ffn_chain.n) if ffn_chain.n < FFN_STEPS else None
                assert attn_chain.n == ATTN_STEPS, attn_chain.n

            attention(0, False)
            with dve.Fori(1, CHUNKS) as c:
                attention(c, True)
            f = CHUNKS - 1
            tail_chain = Chain(dve, ffn_step, FFN_STEPS * f)
            for job in range(J_SLICE0):
                ffn_job(f, job, tail_chain, True)
            for s in range(SLICES):
                ffn_slice(f, s, tail_chain, True)
            take_y(f)
            ffn_job(f, J_Y, tail_chain, True)

        @block.tensor
        def _(pe):
            pe.wait_ge(wqkv_loaded, 16)
            def norm(i):
                pe.wait_ge(squared, i + 1)
                if i >= 2:
                    pe.wait_ge(norms_taken, i - 1)
                if i >= CHUNKS + 2:
                    pe.wait_ge(norms_kept, i - CHUNKS - 1)
                nc.tensor.matmul(banks[0:HEADS, W0 + i % 2, :], head_sum_b[:], squares[:, i % 2, :],
                                 start=True, stop=True).then_inc(norms_filled, 1)

            for i in range(2 * CHUNKS):
                if i < CHUNKS:
                    pe.wait_ge(xT_loaded[i], 16)
                else:
                    pe.wait_ge(parts_ready, i - 3)
                    pe.wait_ge(squared, i - 3)
                w = HID if i < CHUNKS else 0
                nc.tensor.matmul(banks[:, i % 4, :], wqkv_sb[:, w:w + HID],
                                 xT_sb[:, i % CHUNKS * CHUNK:(i % CHUNKS + 1) * CHUNK],
                                 start=True, stop=True).then_inc(projected, 1)
                if i == 1:
                    pe.wait_ge(head_sum_ready, 1)
                if i >= 1:
                    norm(i - 1)
            norm(2 * CHUNKS - 1)
            pe.wait_ge(mean_ready, 1)
            nc.tensor.matmul(banks[0:HEADS, Y, 0:1], head_sum[:], key_mean2[:], start=True, stop=True) \
                .then_inc(mean_filled, 1)
            for k in range(KEY_TILES):
                b = k // 4
                if k % 4 == 0:
                    pe.wait_ge(parts_ready, CHUNKS + b + 1)
                    pe.wait_ge(squared, CHUNKS + b + 1)
                ins = nc.tensor.matmul(banks[:, b, k % 4 * P:(k % 4 + 1) * P], xT_sb[:, k * P:(k + 1) * P],
                                       wqkv_sb[:, 2 * HID:3 * HID], start=True, stop=True)
                if k % 4 == 3:
                    ins.then_inc(v_filled, 1)
            pe.wait_ge(flag_ready, 1)
            pe.wait_ge(values_ready, 4)
            pe.wait_ge(norms_taken, 2 * CHUNKS)
            pe.wait_ge(norms_kept, CHUNKS)
            true_max = pe.value_load(flag_int[0:1, 0:1])
            with pe.If(true_max != 0):
                for half in range(2):
                    pe.wait_ge(keys_loaded[half], KEYS_LOADED)
                    pe.wait_ge(slots_loaded[half], LOADS)
                with pe.Fori(0, CHUNKS) as c:
                    pe.wait_ge(max_chunk_loaded, c + 1)
                    for t in range(TILES):
                        for n in range(HEADS):
                            g, half = n // 2, n % 2
                            rows = slice(half * HALF, half * HALF + SHIFT_ROW)
                            pe.wait_ge(max_taken, c * (TILES * HEADS) + (t * HEADS + n + 1))
                            for k in range(4):
                                ins = nc.tensor.matmul(banks[:, 4 * half + k, :], q_next[rows, g, t * P:(t + 1) * P],
                                                       keys[rows, g, k * CHUNK:(k + 1) * CHUNK], start=True, stop=True)
                            ins.then_inc(max_filled, 1)
                    pe.wait_ge(max_filled, c * (TILES * HEADS) + TILES * HEADS)
                    pe.sem_inc(max_chunk_used, 1)
                pe.wait_ge(max_taken, CHUNKS * TILES * HEADS + 2)

            def scores(c, j):
                u = j // 2
                group, k = u // KEY_TILES, u % KEY_TILES
                g = 2 * group + j % 2
                if k == 0 and j % 2 == 0:
                    pe.wait_ge(q_ready, GROUPS * c + (group + 1))
                if j >= 2 or not isinstance(c, int):
                    pe.wait_ge(exp_done, HALVES * c + (j - 1))
                for half in range(2):
                    rows = slice(half * HALF, half * HALF + ROWS)
                    ins = nc.tensor.matmul(banks[:, 2 * (j % 2) + half, :], keys[rows, g, k * P:(k + 1) * P],
                                           q_now[rows, g, :], start=True, stop=True)
                ins.then_inc(scores_ready, 1)

            def weigh_values(c, u):
                group, k = u // KEY_TILES, u % KEY_TILES
                pe.wait_ge(exp_done, HALVES * c + 2 * (u + 1))
                if k == 0 and (group > 0 or not isinstance(c, int)):
                    pe.wait_ge(acc_taken, GROUPS * c + group)
                for strip in range(4):
                    half, side = strip // 2, strip % 2
                    head = 2 * group + side + PAIRS * half
                    ins = nc.tensor.matmul(banks[32 * strip:32 * strip + 32, ACC, :],
                                           values[:, k, head * VW:head * VW + 32],
                                           probs[:, u % 2, side, half * CHUNK:(half + 1) * CHUNK],
                                           start=(k == 0), stop=(k == KEY_TILES - 1), tile_position=(0, 32 * strip))
                ins.then_inc(pv_done, 1)

            def transpose4(bank, src_of_tile, rows=P):
                for t in range(TILES):
                    ins = nc.tensor.transpose(banks[0:rows, bank, t * P:(t + 1) * P], src_of_tile(t), ident[:])
                return ins

            def untranspose_group(c, group, filled):
                pe.wait_ge(acc_taken, GROUPS * c + (group + 1))
                transpose4(W0, lambda t: heads_raw[:, group, t * P:(t + 1) * P]).then_inc(filled, 1)

            def ffn_job(f, job, c=None):
                freed = FFN_JOBS * (f + 1)
                if job == J_LAST_GROUP:
                    pe.wait_ge(ffn_freed, freed)
                    pe.wait_ge(attn_freed, ATTN_JOBS * (f + 1))
                    untranspose_group(f, GROUPS - 1, ffn_filled)
                elif job == J_ATTN_T:
                    pe.wait_ge(ffn_freed, freed + (J_LAST_GROUP + 1))
                    transpose4(W1, lambda t: attn[:, t, :]).then_inc(ffn_filled, 1)
                elif job == J_PROJ:
                    pe.wait_ge(ffn_freed, freed + (J_ATTN_T + 1))
                    for t in range(TILES):
                        ins = nc.tensor.matmul(banks[:, W0, t * P:(t + 1) * P], attnT[:, t * P:(t + 1) * P], wo_sb[:],
                                               start=True, stop=True)
                    ins.then_inc(ffn_filled, 1)
                elif job == J_X1T:
                    pe.wait_ge(x1_ready, f + 1)
                    transpose4(W1, lambda t: x1[:, t, :]).then_inc(ffn_filled, 1)
                elif job == J_ROUTER:
                    pe.wait_ge(ffn_freed, freed + (J_X1T + 1))
                    for t in range(TILES):
                        ins = nc.tensor.matmul(banks[:, W0, t * EXPERTS:(t + 1) * EXPERTS], x1T[:, t * P:(t + 1) * P],
                                               router_sb[:], start=True, stop=True)
                    ins.then_inc(ffn_filled, 1)
                elif job == J_PROBS_T:
                    pe.wait_ge(h_ready, (SLICES + 1) * f + 1)
                    transpose4(W1, lambda t: route[:, 7, t, :], rows=EXPERTS).then_inc(ffn_filled, 1)
                elif job == J_Y:
                    pe.wait_ge(y_taken, f + 2)
                    pe.wait_ge(ffn_freed, freed + J_Y)
                    transpose4(W0, lambda t: yT[:, t * P:(t + 1) * P]).then_inc(ffn_filled, 1)

            def gate_up(f, s, tail):
                bank = (W0, 0, 2)[s % 3] if tail else W0
                back = 3 if tail and s >= 3 else 1
                if not (tail and s in (1, 2)):
                    pe.wait_ge(ffn_freed, FFN_JOBS * (f + 1) + (J_SLICE0 + s - back + 1))
                if s == 0:
                    pe.wait_ge(weights_loaded, 48)
                for w, b in ((gate_sb, bank), (up_sb, bank + 1)):
                    ins = nc.tensor.matmul(banks[:, b, :], w[:, s * P:(s + 1) * P], x1T[:], start=True, stop=True)
                ins.then_inc(ffn_filled, 1)

            def down(f, s):
                if s == 0:
                    pe.wait_ge(y_taken, f + 1)
                pe.wait_ge(h_ready, (SLICES + 1) * f + (s + 2))
                nc.tensor.matmul(banks[:, Y, :], down_sb[:, s, :], weighted[:, s % 2, :],
                                 start=(s == 0), stop=False).then_inc(down_done, 1)
                if s == SLICES - 1:
                    nc.tensor.matmul(banks[:, Y, :], down_bias[:], routeT[:], start=False, stop=True) \
                        .then_inc(y_filled, 1)

            def attention(c, with_ffn):
                scores(c, 0)
                scores(c, 1)
                for u in range(UNITS):
                    if u + 1 < UNITS:
                        scores(c, 2 * u + 2)
                        scores(c, 2 * u + 3)
                    weigh_values(c, u)
                    if with_ffn:
                        if u in JOB_AT:
                            ffn_job(c - 1, JOB_AT[u])
                        if u in SLICE_AT:
                            s = SLICE_AT.index(u)
                            gate_up(c - 1, s, False)
                            if s:
                                down(c - 1, s - 1)
                        if u == LAST_DOWN_AT:
                            down(c - 1, SLICES - 1)
                        if u == Y_AT:
                            ffn_job(c - 1, J_Y)
                    if u % KEY_TILES == 1 and u > KEY_TILES:
                        if with_ffn:
                            before = sum(a <= u for a in SLICE_AT)
                            pe.wait_ge(ffn_freed, FFN_JOBS * c + (J_SLICE0 + before))
                        elif u > 2 * KEY_TILES:
                            pe.wait_ge(attn_freed, u // KEY_TILES - 1)
                        untranspose_group(c, u // KEY_TILES - 1, attn_filled)
                        if with_ffn:
                            pe.wait_ge(attn_freed, ATTN_JOBS * c + u // KEY_TILES)

            pe.wait_ge(keys_loaded[0], KEYS_LOADED)
            pe.wait_ge(keys_loaded[1], KEYS_LOADED)
            attention(0, False)
            with pe.Fori(1, CHUNKS) as c:
                attention(c, True)
            f = CHUNKS - 1
            for job in range(J_SLICE0):
                ffn_job(f, job)
            for s in range(SLICES):
                gate_up(f, s, True)
                if s >= 2:
                    down(f, s - 2)
            down(f, SLICES - 2)
            down(f, SLICES - 1)
            ffn_job(f, J_Y)


_FORCE_TRUE_MAX = False


def kernel(**inputs):
    import numpy as _np
    import concourse.bacc as _bacc
    from concourse.bass_utils import run_bass_kernel_spmd as _run

    a = {k: _np.asarray(v) for k, v in inputs.items()}
    x = a["L0_attn_x"].reshape(TOKENS, HID)
    arrays = {
        "x": x,
        "xT": x.T,
        "wqkvT": a["L0_attn_w_qkv"].T,
        "woT": a["L0_attn_w_o"].T,
        "routerT": a["L0_ffn_router_w"].T,
        "gate_w": a["L0_ffn_gate_w"],
        "gate_b": a["L0_ffn_gate_b"].reshape(SLICES, P).T,
        "up_w": a["L0_ffn_up_w"],
        "up_b": a["L0_ffn_up_b"].reshape(SLICES, P).T,
        "down_w": a["L0_ffn_down_w"],
        "down_b": a["L0_ffn_down_b"],
        "identity": _np.eye(P, dtype=_np.float32),
        "head_of": _np.kron(_np.eye(HEADS, dtype=_np.float32), _np.ones((D, 1), _np.float32)),
        "rank": _np.tile(_np.arange(EXPERTS, 0, -1, dtype=_np.float32), (P, TILES, 1)),
    }
    arrays = {f"in_{k}": _np.ascontiguousarray(v) for k, v in arrays.items()}
    nc = _bacc.Bacc("TRN2", target_bir_lowering=False, num_devices=1)
    args = [nc.dram_tensor(k, v.shape, mybir.dt.from_np(v.dtype), kind="ExternalInput").ap() for k, v in arrays.items()]
    out = nc.dram_tensor("out", (TOKENS, HID), F32, kind="ExternalOutput").ap()
    build_layer(nc, *args, out, force_true_max=_FORCE_TRUE_MAX)
    r = _run(nc, [arrays], core_ids=[0])
    return r.results[0]["out"].reshape(1, TOKENS, HID)
```

```python
from contextlib import ExitStack

import concourse.bass as bass
from concourse import mybir

F32 = mybir.dt.float32
BF16 = mybir.dt.bfloat16
I32 = mybir.dt.int32
ALU = mybir.AluOpType
ACT = mybir.ActivationFunctionType
AX_X = mybir.AxisListType.X

P = 128
TOKENS = 2048
HID = 128
HEADS = 16
D = HID // HEADS
CHUNK = 512
CHUNKS = TOKENS // CHUNK
TILES = CHUNK // P
KEY_TILES = TOKENS // P
PAIRS = HEADS // 2
GROUPS = HEADS // 4
EXPERTS, D_FF = 8, 256
SLICES = EXPERTS * D_FF // P

SLOT_Q = (0, 1, 2, 0, 1, 0, 1)
SLOT_K = (0, 0, 0, 1, 1, 2, 2)
RUNS = ((0, 3, 0), (3, 2, 1), (5, 2, 2))
SLOTS = len(SLOT_Q)
SHIFT_ROW = SLOTS * D
ROWS = SHIFT_ROW + 3
HALF = 64

VW = D + 1
V_COLS = HEADS * VW + 32 - VW + 1

SCORE_SCALE = float(HID) ** -1.0 * float(D) ** -0.5
OUT_SCALE = (float(HID) ** -0.5) ** 2 * (TOKENS / (TOKENS - 1.0) ** 0.5) * float(TOKENS) ** -0.5
RAISE = 14464.0
REACH = 100.0 / SCORE_SCALE
LN_EPS = 1e-5

UNITS = GROUPS * KEY_TILES
HALVES = 2 * UNITS
ATTN_JOBS = GROUPS - 1
J_LAST_GROUP, J_ATTN_T, J_PROJ, J_X1T, J_ROUTER, J_PROBS_T, J_SLICE0 = range(7)
J_Y = J_SLICE0 + SLICES
FFN_JOBS = J_Y + 1
JOB_AT = {0: J_LAST_GROUP, 1: J_ATTN_T, 2: J_PROJ, 5: J_X1T, 6: J_ROUTER, 9: J_PROBS_T}
GATE_AT = (10, 13, 15, 18, 21, 24, 27, 30, 34, 37, 40, 43, 46, 50, 53, 56)
UP_AT = tuple(u + 1 for u in GATE_AT)
DOWN_AT = (17, 20, 23, 26, 29, 32, 33, 36, 39, 42, 45, 48, 49, 55, 58, 59)
Y_AT = 61
TAIL_BANKS = (0, 2, 5)
TAIL_FIRST = 2
TAIL_LAG = 6
TAIL_BUFFERS = 8
ATTN_STEPS = 3
FFN_STEPS = 55

LOADS = len(RUNS) * 16


def tail_place(job):
    if job < J_PROBS_T or job >= J_SLICE0 + TAIL_FIRST:
        return job + 1
    return J_PROBS_T + TAIL_FIRST + 1 if job == J_PROBS_T else job


class Chain:

    def __init__(self, engine, sem, base):
        self.engine, self.sem, self.base, self.n = engine, sem, base, 0

    def link(self, instruction):
        instruction.then_inc(self.sem, 1)
        self.n += 1
        self.engine.wait_ge(self.sem, self.base + self.n)


def build_layer(nc, x, xT, wqkvT, woT, routerT, gate_w, gate_b, up_w, up_b, down_w, down_b,
                identity, head_of, rank, out):
    with ExitStack() as ctx:
        def sb(name, shape, dt=F32):
            return ctx.enter_context(nc.sbuf_tensor(name, shape, dt))

        def sem(name):
            return ctx.enter_context(nc.semaphore(name))

        xT_sb = sb("xT_sb", [P, TOKENS])
        wqkv_sb = sb("wqkv_sb", [P, 3 * HID])
        wo_sb = sb("wo_sb", [P, HID])
        router_sb = sb("router_sb", [P, EXPERTS])
        ident = sb("ident", [P, P])
        head_sum = sb("head_sum", [P, 32])
        head_sum_b = sb("head_sum_b", [P, 32], BF16)
        rank_sb = sb("rank_sb", [P, TILES, EXPERTS])
        gate_bias = sb("gate_bias", [P, SLICES])
        half_gate_bias = sb("half_gate_bias", [P, SLICES])
        up_bias = sb("up_bias", [P, SLICES])
        down_bias = sb("down_bias", [EXPERTS, HID])
        keys = sb("keys", [P, PAIRS, TOKENS], BF16)
        q_next = sb("q_next", [P, PAIRS, CHUNK], BF16)
        q_now = sb("q_now", [P, PAIRS, CHUNK], BF16)
        values = sb("values", [P, KEY_TILES, V_COLS])
        probs = sb("probs", [P, 2, 2, 2 * CHUNK])
        tail_hidden = probs[:].rearrange("p a b n -> p (a b n)").rearrange("p (i n) -> p i n", i=TAIL_BUFFERS)
        ones = sb("ones", [96, CHUNK], BF16)
        weights = sb("weights", [P, 3 * SLICES * P])
        gate_sb = weights[:, 0:SLICES * P]
        up_sb = weights[:, SLICES * P:2 * SLICES * P]
        down_sb = weights[:, 2 * SLICES * P:3 * SLICES * P].rearrange("p (s d) -> p s d", s=SLICES)
        true_max_rows = weights[0:HEADS, 0:TOKENS]
        q_raw = weights[:, TOKENS:TOKENS + 3 * CHUNK].rearrange("p (i n) -> p i n", i=3)
        squares = weights[:, TOKENS + 3 * CHUNK:TOKENS + 7 * CHUNK].bitcast(BF16) \
            .rearrange("p (i n) -> p i n", i=2 * CHUNKS)
        shift = sb("shift", [P, CHUNK])
        shift_rest = sb("shift_rest", [P, CHUNK])
        shift_parts = sb("shift_parts", [P, 3, CHUNK], BF16)
        shared = sb("shared", [P, 16 * CHUNK])
        parts = shared[:, 0:12 * CHUNK].bitcast(BF16).rearrange("p (i s n) -> p i s n", i=2 * CHUNKS, s=3)
        route_rows = shared[:, 0:8 * CHUNK].rearrange("p (e n) -> p e n", e=EXPERTS)
        gate_tanh = shared[:, 8 * CHUNK:10 * CHUNK].rearrange("p (i n) -> p i n", i=2)
        weighted = shared[:, 12 * CHUNK:16 * CHUNK].rearrange("p (i n) -> p i n", i=4)
        tail_silu = shared[:, 8 * CHUNK:12 * CHUNK].rearrange("p (i n) -> p i n", i=4)
        sigmoid = shared[:, 10 * CHUNK:11 * CHUNK]
        silu = shared[:, 11 * CHUNK:12 * CHUNK]
        rest = sb("rest", [P, 2, CHUNK])
        norm_max = sb("norm_max", [P, 2])
        chunk_max = sb("chunk_max", [HEADS, 2, CHUNKS])
        key_scale = sb("key_scale", [P, 1])
        table_input = sb("table_input", [1, 1])
        table_output = sb("table_output", [1, 2])
        key_sum = sb("key_sum", [P, CHUNKS])
        key_mean = sb("key_mean", [P, 1])
        key_mean2 = sb("key_mean2", [P, 1])
        kq_max = sb("kq_max", [HEADS, 3])
        lengths = sb("lengths", [HEADS, 3])
        key_reach = sb("key_reach", [HEADS, 1])
        square32 = sb("square32", [32, 2, 32])
        flag = sb("flag", [1, 2])
        flag_int = sb("flag_int", [1, 1], I32)
        tile_max = sb("tile_max", [P, 2, 32])
        heads_raw = sb("heads_raw", [P, GROUPS, CHUNK])
        inv_sum = sb("inv_sum", [P, TILES, 4])
        attn = sb("attn", [P, TILES, HID])
        attnT = sb("attnT", [P, CHUNK])
        x_res = sb("x_res", [P, TILES, HID])
        before_ln = sb("before_ln", [P, TILES, HID])
        stats = sb("stats", [P, TILES, 6])
        mean_var = sb("mean_var", [P, TILES, 2])
        var_eps = sb("var_eps", [P, TILES])
        minus_half = sb("minus_half", [P, TILES])
        eps = sb("eps", [P, TILES])
        rstd = sb("rstd", [P, TILES])
        x1 = sb("x1", [P, TILES, HID])
        x1T = sb("x1T", [P, CHUNK])
        small = sb("small", [P, 8, TILES])
        route = sb("route", [P, 8, TILES, EXPERTS])
        routeT = sb("routeT", [EXPERTS, CHUNK])
        half_routeT = sb("half_routeT", [EXPERTS, CHUNK])
        yT = sb("yT", [P, CHUNK])
        result = sb("result", [P, TILES, HID])

        banks = ctx.enter_context(nc.psum_tensor("banks", [P, 8, CHUNK], F32))
        ACC, W0, W1, Y = 4, 5, 6, 7
        ITEM_BANK = (0, 1, 2, 3, 5, 6, 7, 0)
        KEY_NORMS, QUERY_NORMS, MEAN, V_BANKS = 4, 1, 2, (5, 6, 4, 7)

        kq_dram = nc.dram_tensor("kq_parts", [2, 3, D, HEADS, TOKENS], BF16, kind="Internal").ap()
        shift_dram = nc.dram_tensor("shift_rows", [3, HEADS, TOKENS], BF16, kind="Internal").ap()
        route_dram = nc.dram_tensor("route_rows", [EXPERTS, CHUNK], F32, kind="Internal").ap()

        wqkv_loaded, consts_loaded = sem("wqkv_loaded"), sem("consts_loaded")
        xT_loaded = [sem(f"xT_loaded{c}") for c in range(CHUNKS)]
        weights_loaded = sem("weights_loaded")
        projected, squared = sem("projected"), sem("squared")
        parts_ready, norms_filled, q_kept = sem("parts_ready"), sem("norms_filled"), sem("q_kept")
        key_norms_taken, query_norms_taken = sem("key_norms_taken"), sem("query_norms_taken")
        head_sum_loaded, table_ready, key_scale_cleared = sem("head_sum_loaded"), sem("table_ready"), sem("key_scale_cleared")
        key_scale_ready = sem("key_scale_ready")
        head_sum_ready, key_max_ready, bound_ready = sem("head_sum_ready"), sem("key_max_ready"), sem("bound_ready")
        mean_ready, mean_filled, lengths_ready = sem("mean_ready"), sem("mean_filled"), sem("lengths_ready")
        parts_stored = [sem("keys_stored"), sem("queries0_stored"), sem("queries_stored")]
        keys_loaded = [sem("keys_loaded0"), sem("keys_loaded1")]
        other_keys_loaded = [sem("other_keys_loaded0"), sem("other_keys_loaded1")]
        slots_loaded = [sem("slots_loaded0"), sem("slots_loaded1")]
        shift_loaded = [sem("shift_loaded0"), sem("shift_loaded1")]
        values_cleared, v_filled, values_ready = sem("values_cleared"), sem("v_filled"), sem("values_ready")
        ones_ready, flag_ready, shift_ready, max_shift_ready = sem("ones_ready"), sem("flag_ready"), sem("shift_ready"), sem("max_shift_ready")
        shift_stored = [sem("shift0_stored"), sem("shift_stored")]
        q_cleared, shift_zeroed, tile_max_cleared = sem("q_cleared"), sem("shift_zeroed"), sem("tile_max_cleared")
        setup_step, half_bias_ready = sem("setup_step"), sem("half_bias_ready")
        max_filled, max_taken, max_chunk_used, max_q_loaded, max_chunk_loaded, max_step = sem("max_filled"), sem("max_taken"), sem("max_chunk_used"), sem("max_q_loaded"), sem("max_chunk_loaded"), sem("max_step")
        max_stored, max_keys_loaded = sem("max_stored"), sem("max_keys_loaded")
        max_shift_stored, max_shift_loaded = sem("max_shift_stored"), sem("max_shift_loaded")
        scores_ready, exp_done, pv_done, acc_taken = sem("scores_ready"), sem("exp_done"), sem("pv_done"), sem("acc_taken")
        q_ready, attn_filled, attn_freed, attn_step = sem("q_ready"), sem("attn_filled"), sem("attn_freed"), sem("attn_step")
        ffn_filled, ffn_freed, ffn_step = sem("ffn_filled"), sem("ffn_freed"), sem("ffn_step")
        x_loaded, stats_taken, var_ready, eps_added, rstd_ready, x1_ready = sem("x_loaded"), sem("stats_taken"), sem("var_ready"), sem("eps_added"), sem("rstd_ready"), sem("x1_ready")
        logits_ready, router_exp, route_ready, route_stored = sem("logits_ready"), sem("router_exp"), sem("route_ready"), sem("route_stored")
        route_loaded = [sem("first_routes_loaded"), sem("route_loaded")]
        tail_silu_ready, tail_weighted_ready = sem("tail_silu_ready"), sem("tail_weighted_ready")
        gate_filled, tanh_ready, weights_chosen, down_done, y_filled, y_taken = sem("gate_filled"), sem("tanh_ready"), sem("weights_chosen"), sem("down_done"), sem("y_filled"), sem("y_taken")
        result_ready, result_stored = sem("result_ready"), sem("result_stored")

        def load_slots(engine, chunk0, half, done):
            heads = slice(half * PAIRS, (half + 1) * PAIRS)
            for slot, n, _ in RUNS:
                rows = slice(half * HALF + slot * D, half * HALF + (slot + n) * D)
                engine.dma_start(q_next[rows, :, :], kq_dram[1, 0:n, :, heads, bass.ds(chunk0, CHUNK)]
                                 .rearrange("s d g n -> (s d) g n")).then_inc(done, 16)

        def store_shift(engine, c, done):
            engine.dma_start(shift_dram[:, :, c * CHUNK:(c + 1) * CHUNK].rearrange("s h n -> h s n"),
                             shift_parts[32 * c:32 * c + HEADS, :, :]).then_inc(done, 16)

        def load_shift(engine, chunk0, half, done):
            row = half * HALF + SHIFT_ROW
            engine.dma_start(q_next[row:row + 3, :, :],
                             shift_dram[:, half * PAIRS:(half + 1) * PAIRS, bass.ds(chunk0, CHUNK)]) \
                .then_inc(done, 16)

        def load_keys(engine, half, pair0, pair1, done):
            heads = slice(half * PAIRS + pair0, half * PAIRS + pair1)
            for slot, n, part in RUNS:
                rows = slice(half * HALF + slot * D, half * HALF + (slot + n) * D)
                src = kq_dram[0, part, :, heads, :].rearrange("d g n -> d (g n)")
                engine.dma_start(keys[rows, pair0:pair1, :].rearrange("r g n -> r (g n)"),
                                 src.unsqueeze(0).broadcast_to([n, D, (pair1 - pair0) * TOKENS])).then_inc(done, 16)

        def load_ones(engine, half):
            row = half * HALF + SHIFT_ROW
            engine.dma_start(keys[row:row + 3, :, :].rearrange("r g (b n) -> r (g b) n", n=CHUNK), ones[:]) \
                .then_inc(keys_loaded[half], 16)

        def score_bank(c, j):
            if isinstance(c, int) and j < HALVES:
                return (0, 2, W0)[j % 3]
            return 2 * (j % 2)

        CONSTS_LOADED = 7 * 16
        KEYS_LOADED = 16 + LOADS

        def store_parts(engine, i, done):
            engine.wait_ge(parts_ready, i + 1)
            cols = slice(i % CHUNKS * CHUNK, (i % CHUNKS + 1) * CHUNK)
            engine.dma_start(kq_dram[i // CHUNKS, :, :, :, cols].rearrange("s d h n -> (d h) s n"),
                             parts[:, i, :, :]).then_inc(done, 16)

        block = ctx.enter_context(nc.Block())

        @block.sync
        def _(sp):
            sp.dma_start(wqkv_sb[:], wqkvT).then_inc(wqkv_loaded, 16)
            for c in range(CHUNKS):
                cols = slice(c * CHUNK, (c + 1) * CHUNK)
                sp.dma_start(xT_sb[:, cols], xT[:, cols]).then_inc(xT_loaded[c], 16)
                if c == 0:
                    sp.dma_start(head_sum[:], head_of).then_inc(head_sum_loaded, 16)
            sp.wait_ge(ones_ready, 1)
            load_ones(sp, 0)
            for i in range(CHUNKS):
                store_parts(sp, i, parts_stored[0])
            store_parts(sp, CHUNKS, parts_stored[1])
            sp.wait_ge(parts_stored[0], CHUNKS * 16)
            load_keys(sp, 0, 0, 2, keys_loaded[0])
            sp.wait_ge(shift_ready, 1)
            store_shift(sp, 0, shift_stored[0])
            sp.wait_ge(parts_stored[1], 16)
            sp.wait_ge(q_cleared, 1)
            load_slots(sp, 0, 0, slots_loaded[0])
            sp.wait_ge(shift_stored[0], 16)
            load_shift(sp, 0, 0, shift_loaded[0])
            sp.wait_ge(flag_ready, 1)
            true_max = sp.value_load(flag_int[0:1, 0:1])
            with sp.If(true_max != 0):
                load_keys(sp, 0, 2, PAIRS, max_keys_loaded)
                for i in range(CHUNKS + 1, 2 * CHUNKS):
                    store_parts(sp, i, max_stored)
                sp.wait_ge(max_keys_loaded, LOADS)
                sp.wait_ge(max_stored, (CHUNKS - 1) * 16)
                sp.wait_ge(slots_loaded[0], LOADS)
                sp.wait_ge(slots_loaded[1], LOADS)
                sp.sem_inc(max_chunk_loaded, 1)
                for n, c in enumerate((1, 2, 3, 0)):
                    sp.wait_ge(max_chunk_used, n + 1)
                    load_slots(sp, c * CHUNK, 0, max_q_loaded)
                    load_slots(sp, c * CHUNK, 1, max_q_loaded)
                    sp.wait_ge(max_q_loaded, (n + 1) * 2 * LOADS)
                    sp.sem_inc(max_chunk_loaded, 1)
                sp.wait_ge(max_shift_ready, 1)
                store_shift(sp, 0, max_shift_stored)
                sp.wait_ge(max_shift_stored, 16)
                for half in range(2):
                    sp.wait_ge(shift_loaded[half], 16)
                    load_shift(sp, 0, half, max_shift_loaded)
            for c in range(1, CHUNKS):
                store_shift(sp, c, shift_stored[1])
            load_keys(sp, 0, 2, PAIRS, other_keys_loaded[0])
            for i in range(CHUNKS + 1, 2 * CHUNKS):
                store_parts(sp, i, parts_stored[2])
            for dst, src in ((ident[:], identity), (wo_sb[:], woT), (router_sb[:], routerT), (rank_sb[:], rank),
                             (gate_bias[:], gate_b), (up_bias[:], up_b), (down_bias[:], down_b)):
                sp.dma_start(dst, src).then_inc(consts_loaded, 16)
            sp.dma_start(x_res[:], x[0:CHUNK, :].rearrange("(t p) c -> p t c", p=P)).then_inc(x_loaded, 16)
            sp.wait_ge(parts_stored[2], (CHUNKS - 1) * 16)
            sp.wait_ge(shift_stored[1], (CHUNKS - 1) * 16)
            sp.dma_start(gate_sb.rearrange("p (e f) -> p e f", e=EXPERTS), gate_w.rearrange("e p f -> p e f")) \
                .then_inc(weights_loaded, 16)
            sp.dma_start(up_sb.rearrange("p (e f) -> p e f", e=EXPERTS), up_w.rearrange("e p f -> p e f")) \
                .then_inc(weights_loaded, 16)
            sp.dma_start(down_sb, down_w.rearrange("e (s p) d -> p (e s) d", p=P)).then_inc(weights_loaded, 16)

            def next_queries(c, chunk):
                sp.wait_ge(q_ready, GROUPS * (c + 1))
                load_slots(sp, chunk * CHUNK, 0, slots_loaded[0])
                load_shift(sp, chunk * CHUNK, 0, shift_loaded[0])

            def route_and_result(f):
                sp.wait_ge(route_ready, f + 1)
                sp.dma_start(route_dram, half_routeT[:]).then_inc(route_stored, 16)
                sp.wait_ge(route_stored, 16 * (f + 1))
                for i, experts in enumerate((slice(0, 2), slice(2, EXPERTS))):
                    sp.dma_start(route_rows[:, experts, :], route_dram[experts, :].partition_broadcast(P)) \
                        .then_inc(route_loaded[i], 16)
                sp.wait_ge(result_ready, TILES * (f + 1))
                sp.dma_start(out[bass.ds(f * CHUNK, CHUNK), :].rearrange("(t p) c -> p t c", p=P),
                             result[:]).then_inc(result_stored, 16)

            def next_x(f):
                sp.wait_ge(stats_taken, 2 * f - 1)
                sp.dma_start(x_res[:], x[bass.ds(f * CHUNK, CHUNK), :].rearrange("(t p) c -> p t c", p=P)) \
                    .then_inc(x_loaded, 16)

            next_queries(0, 1)
            with sp.Fori(1, CHUNKS) as c:
                next_queries(c, (c + 1) % CHUNKS)
                route_and_result(c - 1)
                next_x(c)
            route_and_result(CHUNKS - 1)
            sp.wait_ge(result_stored, 16 * (CHUNKS + 1))

        @block.gpsimd
        def _(pool):
            nc.gpsimd.memset(table_input[:], 0.0).then_inc(table_ready, 1)
            nc.gpsimd.memset(key_scale[:], 0.0).then_inc(key_scale_cleared, 1)
            nc.gpsimd.memset(ones[:], 1.0).then_inc(ones_ready, 1)
            nc.gpsimd.memset(q_next[:], 0.0).then_inc(q_cleared, 1)
            pool.wait_ge(ones_ready, 1)
            load_ones(pool, 1)
            nc.gpsimd.memset(shift_parts[:, 1, :], RAISE)
            nc.gpsimd.memset(shift_parts[:, 2, :], 0.0).then_inc(shift_zeroed, 1)
            nc.gpsimd.memset(square32[:], 0.0)
            nc.gpsimd.memset(minus_half[:], -0.5)
            nc.gpsimd.memset(eps[:], LN_EPS)
            nc.gpsimd.memset(tile_max[:], 0.0).then_inc(tile_max_cleared, 1)
            nc.gpsimd.memset(values[:], 0.0).then_inc(values_cleared, 1)
            pool.wait_ge(values_cleared, 1)
            nc.gpsimd.memset(values[:, :, 0:HEADS * VW].rearrange("p k (h v) -> p k h v", v=VW)[:, :, :, D:VW], 1.0) \
                .then_inc(values_cleared, 1)
            pool.wait_ge(parts_stored[0], CHUNKS * 16)
            load_keys(pool, 1, 0, 2, keys_loaded[1])
            pool.wait_ge(parts_stored[1], 16)
            pool.wait_ge(q_cleared, 1)
            load_slots(pool, 0, 1, slots_loaded[1])
            pool.wait_ge(shift_stored[0], 16)
            load_shift(pool, 0, 1, shift_loaded[1])
            load_keys(pool, 1, 2, PAIRS, other_keys_loaded[1])
            pool.wait_ge(parts_stored[2], (CHUNKS - 1) * 16)
            pool.wait_ge(shift_stored[1], (CHUNKS - 1) * 16)

            def next_queries(c, chunk):
                pool.wait_ge(q_ready, GROUPS * (c + 1))
                load_slots(pool, chunk * CHUNK, 1, slots_loaded[1])
                load_shift(pool, chunk * CHUNK, 1, shift_loaded[1])

            def norms(f):
                for n in range(2):
                    pool.wait_ge(var_ready, 2 * f + n + 1)
                    nc.gpsimd.tensor_tensor(var_eps[:], mean_var[:, :, 1], eps[:], ALU.add).then_inc(eps_added, 1)
                    pool.wait_ge(eps_added, 2 * f + n + 1)
                    nc.gpsimd.tensor_tensor(rstd[:], var_eps[:], minus_half[:], ALU.pow).then_inc(rstd_ready, 1)

            next_queries(0, 1)
            with pool.Fori(1, CHUNKS) as c:
                next_queries(c, (c + 1) % CHUNKS)
                norms(c - 1)
            norms(CHUNKS - 1)

        @block.scalar
        def _(act):
            act.wait_ge(table_ready, 1)
            nc.scalar.activation(table_output[:, 0:1], table_input[:], ACT.Sqrt)
            for i in range(2 * CHUNKS):
                act.wait_ge(projected, i + 1)
                bank = banks[:, ITEM_BANK[i], :]
                nc.scalar.activation(parts[:, i, 0, :], bank, ACT.Copy,
                                     accum_out=key_sum[:, i:i + 1] if i < CHUNKS else None)
                nc.scalar.activation(squares[:, i, :], bank, ACT.Square).then_inc(squared, 1)
                if i > CHUNKS:
                    nc.scalar.copy(q_raw[:, i - CHUNKS - 1, :], bank).then_inc(q_kept, 1)
            act.wait_ge(key_scale_ready, 1)
            act.wait_ge(query_norms_taken, 1)
            nc.scalar.activation(shift[:], banks[:, QUERY_NORMS, :], ACT.Sqrt, scale=key_scale[:]).then_inc(bound_ready, 1)
            act.wait_ge(key_max_ready, 1)
            nc.scalar.activation(lengths[:], kq_max[:], ACT.Sqrt).then_inc(lengths_ready, 1)
            act.wait_ge(lengths_ready, 1)
            nc.scalar.activation(table_output[:, 1:2], table_input[:], ACT.Exp)

            def exp_half(c, j):
                u = j // 2
                act.wait_ge(scores_ready, HALVES * c + (j + 1))
                if u >= 2 or not isinstance(c, int):
                    act.wait_ge(pv_done, UNITS * c + (u - 1))
                pair = score_bank(c, j)
                nc.scalar.activation(probs[:, u % 2, j % 2, :], banks[:, pair:pair + 2, :].rearrange("p b n -> p (b n)"),
                                     ACT.Exp, scale=SCORE_SCALE).then_inc(exp_done, 1)

            def router_exp_step(f):
                act.wait_ge(logits_ready, f + 1)
                nc.scalar.activation(route[:, 1], route[:, 0], ACT.Exp).then_inc(router_exp, 1)

            def gate_step(f, s):
                act.wait_ge(gate_filled, SLICES * f + (s + 1))
                if s >= 2:
                    act.wait_ge(ffn_freed, FFN_JOBS * (f + 1) + (J_SLICE0 + s - 1))
                nc.scalar.activation(gate_tanh[:, s % 2, :], banks[:, W0, :], ACT.Tanh,
                                     bias=half_gate_bias[:, s:s + 1], scale=0.5).then_inc(tanh_ready, 1)

            def tail_gate_step(f, s):
                act.wait_ge(gate_filled, SLICES * f + (s + 1))
                if s >= 4:
                    act.wait_ge(ffn_freed, FFN_JOBS * (f + 1) + tail_place(J_SLICE0 + s - 4))
                nc.scalar.activation(tail_silu[:, s % 4, :], banks[:, TAIL_BANKS[s % 3], :], ACT.Silu,
                                     bias=gate_bias[:, s:s + 1]).then_inc(tail_silu_ready, 1)

            def attention(c, with_ffn):
                for u in range(UNITS):
                    exp_half(c, 2 * u)
                    exp_half(c, 2 * u + 1)
                    if with_ffn:
                        if JOB_AT.get(u - 1) == J_ROUTER:
                            router_exp_step(c - 1)
                        if u - 1 in GATE_AT:
                            gate_step(c - 1, GATE_AT.index(u - 1))

            attention(0, False)
            act.wait_ge(consts_loaded, CONSTS_LOADED)
            nc.scalar.mul(half_gate_bias[:], gate_bias[:], 0.5).then_inc(half_bias_ready, 1)
            act.wait_ge(half_bias_ready, 1)
            with act.Fori(1, CHUNKS) as c:
                attention(c, True)
            router_exp_step(CHUNKS - 1)
            for s in range(SLICES):
                tail_gate_step(CHUNKS - 1, s)

        @block.vector
        def _(dve):
            chain = Chain(dve, setup_step, 0)

            dve.wait_ge(head_sum_loaded, 16)
            nc.vector.tensor_copy(head_sum_b[:], head_sum[:]).then_inc(head_sum_ready, 1)

            def split(i):
                if i <= CHUNKS:
                    dve.wait_ge(squared, i + 1)
                    whole = banks[:, ITEM_BANK[i], :]
                else:
                    dve.wait_ge(q_kept, i - CHUNKS)
                    whole = q_raw[:, i - CHUNKS - 1, :]
                chain.link(nc.vector.tensor_tensor(rest[:, i % 2, :], whole, parts[:, i, 0, :], ALU.subtract))
                chain.link(nc.vector.tensor_copy(parts[:, i, 1, :], rest[:, i % 2, :]))
                nc.vector.tensor_tensor(parts[:, i, 2, :], rest[:, i % 2, :], parts[:, i, 1, :], ALU.subtract) \
                    .then_inc(parts_ready, 1)

            def combine_chunks(which):
                for c in range(CHUNKS):
                    copy = nc.vector.tensor_copy(chunk_max[:, which, c:c + 1],
                                                 norm_max[32 * c:32 * c + HEADS, which:which + 1])
                chain.link(copy)
                return nc.vector.tensor_reduce(kq_max[:, which:which + 1], chunk_max[:, which, :], AX_X, ALU.max)

            for i in range(CHUNKS):
                split(i)
            chain.link(nc.vector.tensor_reduce(key_mean[:], key_sum[:], AX_X, ALU.add))
            nc.vector.scalar_tensor_tensor(out=key_mean2[:], in0=key_mean[:], scalar=1.0 / TOKENS ** 2,
                                           in1=key_mean[:], op0=ALU.mult, op1=ALU.mult).then_inc(mean_ready, 1)
            split(CHUNKS)
            dve.wait_ge(norms_filled, CHUNKS)
            nc.vector.tensor_reduce(norm_max[:, 0:1], banks[:, KEY_NORMS, :], AX_X, ALU.max).then_inc(key_norms_taken, 1)
            dve.wait_ge(key_norms_taken, 1)
            chain.link(combine_chunks(0))
            dve.wait_ge(key_scale_cleared, 1)
            for c in range(CHUNKS):
                copy = nc.vector.tensor_copy(key_scale[32 * c:32 * c + HEADS, :], kq_max[:, 0:1])
            copy.then_inc(key_scale_ready, 1)
            dve.wait_ge(norms_filled, 2 * CHUNKS)
            nc.vector.tensor_reduce(norm_max[:, 1:2], banks[:, QUERY_NORMS, :], AX_X, ALU.max) \
                .then_inc(query_norms_taken, 1)
            dve.wait_ge(query_norms_taken, 1)
            chain.link(combine_chunks(1))
            dve.wait_ge(mean_filled, 1)
            nc.vector.tensor_copy(kq_max[:, 2:3], banks[0:HEADS, MEAN, 0:1]).then_inc(key_max_ready, 1)
            dve.wait_ge(bound_ready, 1)
            dve.wait_ge(shift_zeroed, 1)
            nc.vector.tensor_scalar(shift_parts[:, 0, :], shift[:], RAISE, -1.0, ALU.max, ALU.mult) \
                .then_inc(shift_ready, 1)
            dve.wait_ge(lengths_ready, 1)
            dve.wait_ge(tile_max_cleared, 1)
            chain.link(nc.vector.tensor_tensor(key_reach[:], lengths[:, 0:1], lengths[:, 2:3], ALU.add))
            chain.link(nc.vector.tensor_tensor(square32[0:HEADS, 0, 0:1], key_reach[:], lengths[:, 1:2], ALU.mult))
            chain.link(nc.vector.transpose(square32[:, 1, :], square32[:, 0, :]))
            chain.link(nc.vector.tensor_reduce(flag[0:1, 0:1], square32[0:1, 1, 0:HEADS], AX_X, ALU.max))
            nc.vector.tensor_scalar(flag_int[0:1, 0:1], flag[0:1, 0:1], REACH, None, ALU.is_gt) \
                .then_inc(flag_ready, 1)
            for i in range(CHUNKS + 1, 2 * CHUNKS):
                split(i)
            dve.wait_ge(flag_ready, 1)
            true_max = dve.value_load(flag_int[0:1, 0:1])
            with dve.If(true_max != 0):
                dve.sem_inc(max_taken, 2)
                with dve.Fori(0, CHUNKS) as c:
                    per_chunk = TILES * HEADS
                    steps = Chain(dve, max_step, c * (TILES * 2))
                    for t in range(TILES):
                        for n in range(HEADS):
                            dve.wait_ge(max_filled, c * per_chunk + (t * HEADS + n + 1))
                            head = n // 2 + PAIRS * (n % 2)
                            reduce = nc.vector.tensor_reduce(
                                tile_max[:, 0, head:head + 1], banks[:, 4 * (n % 2):4 * (n % 2) + 4, :], mybir.AxisListType.XY, ALU.max)
                            reduce.then_inc(max_taken, 1)
                        dve.wait_ge(max_taken, c * per_chunk + (t * HEADS + HEADS + 2))
                        steps.link(nc.vector.transpose(tile_max[:, 1, :], tile_max[:, 0, :]))
                        for b in range(4):
                            copy = nc.vector.tensor_copy(true_max_rows[:, bass.ds(c * CHUNK + (t * P + b * 32), 32)],
                                                         tile_max[32 * b:32 * b + HEADS, 1, :])
                        steps.link(copy)
                steps = Chain(dve, max_step, CHUNKS * TILES * 2)
                dve.wait_ge(shift_ready, 1)
                dve.wait_ge(shift_stored[0], 16)
                for c in range(CHUNKS):
                    copy = nc.vector.tensor_copy(shift[32 * c:32 * c + HEADS, :], true_max_rows[:, c * CHUNK:(c + 1) * CHUNK])
                steps.link(copy)
                steps.link(nc.vector.tensor_scalar(shift_parts[:, 0, :], shift[:], -1.0, None, ALU.mult))
                steps.link(nc.vector.scalar_tensor_tensor(out=shift_rest[:], in0=shift[:], scalar=-1.0,
                                                          in1=shift_parts[:, 0, :], op0=ALU.mult, op1=ALU.subtract))
                steps.link(nc.vector.tensor_copy(shift_parts[:, 1, :], shift_rest[:]))
                nc.vector.tensor_tensor(shift_parts[:, 2, :], shift_rest[:], shift_parts[:, 1, :], ALU.subtract) \
                    .then_inc(max_shift_ready, 1)
                dve.wait_ge(max_q_loaded, 4 * 2 * LOADS)
                dve.wait_ge(max_shift_loaded, 2 * 16)

            def copy_queries(group):
                pairs = slice(2 * group, 2 * group + 2)
                nc.vector.tensor_copy(q_now[:, pairs, :], q_next[:, pairs, :]).then_inc(q_ready, 1)

            def queries_loaded(chunks):
                for half in range(2):
                    dve.wait_ge(slots_loaded[half], LOADS * chunks)
                    dve.wait_ge(shift_loaded[half], 16 * chunks)

            dve.sem_inc(ffn_freed, FFN_JOBS)
            dve.sem_inc(down_done, 4)
            dve.sem_inc(y_taken, 1)
            dve.sem_inc(result_stored, 16)
            dve.wait_ge(values_cleared, 2)
            for b in range(4):
                if b == 1:
                    queries_loaded(1)
                    copy_queries(0)
                dve.wait_ge(v_filled, b + 1)
                nc.vector.tensor_copy(
                    values[:, 4 * b:4 * b + 4, 0:HEADS * VW].rearrange("p k (h v) -> p k h v", v=VW)[:, :, :, 0:D],
                    banks[:, V_BANKS[b], :].rearrange("p (k h d) -> p k h d", k=4, d=D)).then_inc(values_ready, 1)
            for group in range(1, GROUPS):
                copy_queries(group)

            def normalise(group, freed, chain, bank=W0):
                raw = banks[:, bank, :].rearrange("p (t h v) -> p t h v", t=TILES, v=32)
                chain.link(nc.vector.reciprocal(inv_sum[:].unsqueeze(3), raw[:, :, :, D:VW]))
                for half in range(2):
                    c0 = half * HALF + 2 * D * group
                    ins = nc.vector.tensor_tensor(
                        attn[:, :, c0:c0 + 2 * D].rearrange("p t (h d) -> p t h d", d=D),
                        raw[:, :, 2 * half:2 * half + 2, 0:D],
                        inv_sum[:, :, 2 * half:2 * half + 2].unsqueeze(3).broadcast_to([P, TILES, 2, D]), ALU.mult)
                ins.then_inc(freed, 1)

            def layernorm(f, which, dst, chain, ready):
                for t in range(TILES):
                    ins = nc.vector.bn_stats(stats[:, t, :], before_ln[:, t, :])
                chain.link(ins)
                dve.sem_inc(stats_taken, 1)
                for t in range(TILES):
                    ins = nc.vector.bn_aggr(mean_var[:, t, :], stats[:, t, :])
                ins.then_inc(var_ready, 1)
                dve.wait_ge(rstd_ready, 2 * f + which + 1)
                dve.wait_ge(var_ready, 2 * f + which + 1)
                for t in range(TILES):
                    nc.vector.tensor_scalar(dst[:, t, :], before_ln[:, t, :], mean_var[:, t, 0:1], rstd[:, t:t + 1],
                                            ALU.subtract, ALU.mult).then_inc(ready, 1)

            def ffn_job(f, job, chain, tail):
                dve.wait_ge(ffn_filled, FFN_JOBS * f + (tail_place(job) if tail else job + 1))
                w0, w1 = banks[:, W0, :], banks[:, W1, :]
                if job == J_LAST_GROUP:
                    normalise(GROUPS - 1, ffn_freed, chain)
                elif job == J_ATTN_T:
                    nc.vector.tensor_copy(attnT[:], w1).then_inc(ffn_freed, 1)
                elif job == J_PROJ:
                    dve.wait_ge(x_loaded, 16 * (f + 1))
                    ins = nc.vector.scalar_tensor_tensor(
                        out=before_ln[:].rearrange("p t c -> p (t c)"), in0=w0, scalar=OUT_SCALE,
                        in1=x_res[:].rearrange("p t c -> p (t c)"), op0=ALU.mult, op1=ALU.add)
                    ins.then_inc(ffn_freed, 1)
                    dve.wait_ge(ffn_freed, FFN_JOBS * (f + 1) + (job + 1))
                    layernorm(f, 0, x1, chain, x1_ready)
                elif job == J_X1T:
                    nc.vector.tensor_copy(x1T[:], w1).then_inc(ffn_freed, 1)
                elif job == J_ROUTER:
                    router(f, chain)
                elif job == J_PROBS_T:
                    probsT = banks[0:EXPERTS, ACC if tail else W1, :]
                    nc.vector.tensor_scalar(half_routeT[:], probsT, 0.5, None, ALU.mult).then_inc(route_ready, 1)
                    nc.vector.tensor_copy(routeT[:], probsT).then_inc(ffn_freed, 1)
                elif job == J_Y:
                    nc.vector.tensor_tensor(before_ln[:].rearrange("p t c -> p (t c)"), w0,
                                            x1[:].rearrange("p t c -> p (t c)"), ALU.add).then_inc(ffn_freed, 1)
                    dve.wait_ge(ffn_freed, FFN_JOBS * (f + 1) + (job + 1))
                    dve.wait_ge(result_stored, 16 * (f + 1))
                    layernorm(f, 1, result, chain, result_ready)

            def router(f, chain):
                logits = banks[:, W0, 0:TILES * EXPERTS].rearrange("p (t e) -> p t e", e=EXPERTS)

                def wide(column):
                    return small[:, column, :].unsqueeze(2).broadcast_to([P, TILES, EXPERTS])

                def reduce(column, src, op):
                    chain.link(nc.vector.tensor_reduce(small[:, column, :], src, AX_X, op))

                def elementwise(dst, a, b, op):
                    chain.link(nc.vector.tensor_tensor(route[:, dst], a, b, op))

                reduce(0, logits, ALU.max)
                nc.vector.tensor_tensor(route[:, 0], logits, wide(0), ALU.subtract).then_inc(ffn_freed, 1)
                dve.wait_ge(ffn_freed, FFN_JOBS * (f + 1) + (J_ROUTER + 1))
                dve.sem_inc(logits_ready, 1)
                dve.wait_ge(router_exp, f + 1)
                reduce(1, route[:, 1], ALU.add)
                chain.link(nc.vector.reciprocal(small[:, 2, :], small[:, 1, :]))
                elementwise(2, route[:, 1], wide(2), ALU.mult)
                reduce(3, route[:, 2], ALU.max)
                elementwise(3, route[:, 2], wide(3), ALU.is_equal)
                elementwise(3, route[:, 3], rank_sb[:], ALU.mult)
                reduce(4, route[:, 3], ALU.max)
                elementwise(4, rank_sb[:], wide(4), ALU.is_equal)
                chain.link(nc.vector.scalar_tensor_tensor(
                    out=route[:, 5], in0=route[:, 4], scalar=-2.0, in1=route[:, 2], op0=ALU.mult, op1=ALU.add))
                reduce(3, route[:, 5], ALU.max)
                elementwise(3, route[:, 5], wide(3), ALU.is_equal)
                elementwise(3, route[:, 3], rank_sb[:], ALU.mult)
                reduce(4, route[:, 3], ALU.max)
                elementwise(6, rank_sb[:], wide(4), ALU.is_equal)
                elementwise(6, route[:, 6], route[:, 4], ALU.add)
                elementwise(6, route[:, 6], route[:, 2], ALU.mult)
                reduce(5, route[:, 6], ALU.add)
                chain.link(nc.vector.tensor_scalar(small[:, 6, :], small[:, 5, :], 1e-9, None, ALU.add))
                chain.link(nc.vector.reciprocal(small[:, 7, :], small[:, 6, :]))
                nc.vector.tensor_tensor(route[:, 7], route[:, 6], wide(7), ALU.mult).then_inc(weights_chosen, 1)

            def ffn_slice(f, s, chain):
                gate, up = banks[:, W0, :], banks[:, W1, :]
                if s in (0, 4):
                    dve.wait_ge(route_loaded[s // 4], 16 * (f + 1))
                dve.wait_ge(tanh_ready, SLICES * f + (s + 1))
                chain.link(nc.vector.scalar_tensor_tensor(out=sigmoid, in0=gate_tanh[:, s % 2, :], scalar=1.0,
                                                          in1=route_rows[:, s // 2, :], op0=ALU.add, op1=ALU.mult))
                dve.wait_ge(ffn_filled, FFN_JOBS * f + (J_SLICE0 + s + 1))
                chain.link(nc.vector.scalar_tensor_tensor(out=silu, in0=gate, scalar=gate_bias[:, s:s + 1],
                                                          in1=sigmoid, op0=ALU.add, op1=ALU.mult))
                dve.wait_ge(down_done, SLICES * f + (s + 1))
                nc.vector.scalar_tensor_tensor(out=weighted[:, s % 4, :], in0=up, scalar=up_bias[:, s:s + 1], in1=silu,
                                               op0=ALU.add, op1=ALU.mult).then_inc(ffn_freed, 1)

            def tail_hidden_step(f, s):
                if s >= TAIL_BUFFERS:
                    dve.wait_ge(down_done, SLICES * f + 4 + (s - TAIL_BUFFERS + 1))
                dve.wait_ge(tail_silu_ready, s + 1)
                dve.wait_ge(ffn_filled, FFN_JOBS * f + tail_place(J_SLICE0 + s))
                nc.vector.scalar_tensor_tensor(
                    out=tail_hidden[:, s % TAIL_BUFFERS, :], in0=banks[:, TAIL_BANKS[s % 3] + 1, :],
                    scalar=up_bias[:, s:s + 1], in1=tail_silu[:, s % 4, :], op0=ALU.add, op1=ALU.mult) \
                    .then_inc(ffn_freed, 1)

            def tail_weigh_step(f, s):
                if s in (0, 4):
                    dve.wait_ge(route_loaded[s // 4], 16 * (f + 1))
                dve.wait_ge(ffn_freed, FFN_JOBS * (f + 1) + tail_place(J_SLICE0 + s))
                hidden = tail_hidden[:, s % TAIL_BUFFERS, :]
                nc.vector.scalar_tensor_tensor(out=hidden, in0=hidden, scalar=2.0, in1=route_rows[:, s // 2, :],
                                               op0=ALU.mult, op1=ALU.mult).then_inc(tail_weighted_ready, 1)

            def take_y(f):
                dve.wait_ge(y_filled, f + 1)
                nc.vector.tensor_copy(yT[:], banks[:, Y, :]).then_inc(y_taken, 1)

            def attention(c, with_ffn):
                attn_chain = Chain(dve, attn_step, ATTN_STEPS * c)
                ffn_chain = Chain(dve, ffn_step, FFN_STEPS * (c - 1)) if with_ffn else None
                for u in range(UNITS):
                    if with_ffn:
                        if u in JOB_AT:
                            ffn_job(c - 1, JOB_AT[u], ffn_chain, False)
                        if u - 1 in UP_AT:
                            ffn_slice(c - 1, UP_AT.index(u - 1), ffn_chain)
                        if u == Y_AT - 1:
                            take_y(c - 1)
                        if u == Y_AT + 1:
                            ffn_job(c - 1, J_Y, ffn_chain, False)
                    if u % KEY_TILES == 1 and u > KEY_TILES:
                        dve.wait_ge(attn_filled, ATTN_JOBS * c + u // KEY_TILES)
                        normalise(u // KEY_TILES - 1, attn_freed, attn_chain, W0 if with_ffn else Y)
                    if u % KEY_TILES == KEY_TILES - 1:
                        group = u // KEY_TILES
                        dve.wait_ge(scores_ready, HALVES * c + 2 * (u + 1))
                        if group == 0:
                            queries_loaded(c + 2)
                        if group < GROUPS - 1:
                            copy_queries(group)
                        dve.wait_ge(pv_done, UNITS * c + (u + 1))
                        nc.vector.tensor_copy(heads_raw[:, group, :], banks[:, ACC, :]).then_inc(acc_taken, 1)
                        if group == GROUPS - 1:
                            copy_queries(group)
                if with_ffn:
                    assert ffn_chain.n == FFN_STEPS, ffn_chain.n
                assert attn_chain.n == ATTN_STEPS, attn_chain.n

            attention(0, False)
            dve.wait_ge(consts_loaded, CONSTS_LOADED)
            with dve.Fori(1, CHUNKS) as c:
                attention(c, True)
            f = CHUNKS - 1
            tail_chain = Chain(dve, ffn_step, FFN_STEPS * f)
            for job in range(J_PROBS_T):
                ffn_job(f, job, tail_chain, True)
            for s in range(SLICES + TAIL_LAG):
                if s == TAIL_FIRST:
                    ffn_job(f, J_PROBS_T, tail_chain, True)
                if s >= TAIL_LAG:
                    tail_weigh_step(f, s - TAIL_LAG)
                if s < SLICES:
                    tail_hidden_step(f, s)
            take_y(f)
            ffn_job(f, J_Y, tail_chain, True)

        @block.tensor
        def _(pe):
            pe.wait_ge(wqkv_loaded, 16)
            def project(i):
                if i < CHUNKS:
                    pe.wait_ge(xT_loaded[i], 16)
                w = HID if i < CHUNKS else 0
                nc.tensor.matmul(banks[:, ITEM_BANK[i], :], wqkv_sb[:, w:w + HID],
                                 xT_sb[:, i % CHUNKS * CHUNK:(i % CHUNKS + 1) * CHUNK],
                                 start=True, stop=True).then_inc(projected, 1)

            def norm(i):
                pe.wait_ge(squared, i + 1)
                row = 32 * (i % CHUNKS)
                nc.tensor.matmul(banks[row:row + 32, KEY_NORMS if i < CHUNKS else QUERY_NORMS, :], head_sum_b[:],
                                 squares[:, i, :], start=True, stop=True, tile_position=(0, row)).then_inc(norms_filled, 1)

            for i in range(2 * CHUNKS - 1):
                project(i)
            pe.wait_ge(parts_ready, 1)
            project(2 * CHUNKS - 1)
            pe.wait_ge(head_sum_ready, 1)
            for i in range(CHUNKS):
                norm(i)
            pe.wait_ge(parts_ready, 2)
            for i in range(CHUNKS, 2 * CHUNKS):
                norm(i)
            pe.wait_ge(mean_ready, 1)
            pe.wait_ge(parts_ready, 3)
            nc.tensor.matmul(banks[0:32, MEAN, 0:1], head_sum[:], key_mean2[:], start=True, stop=True) \
                .then_inc(mean_filled, 1)
            pe.wait_ge(flag_ready, 1)
            pe.wait_ge(q_kept, 3)
            pe.wait_ge(shift_ready, 1)
            true_max = pe.value_load(flag_int[0:1, 0:1])
            with pe.If(true_max != 0):
                for half in range(2):
                    pe.wait_ge(keys_loaded[half], KEYS_LOADED)
                pe.wait_ge(max_keys_loaded, LOADS)
                pe.wait_ge(other_keys_loaded[1], LOADS)
                with pe.Fori(0, CHUNKS) as c:
                    pe.wait_ge(max_chunk_loaded, c + 1)
                    for t in range(TILES):
                        for n in range(HEADS):
                            g, half = n // 2, n % 2
                            rows = slice(half * HALF, half * HALF + SHIFT_ROW)
                            pe.wait_ge(max_taken, c * (TILES * HEADS) + (t * HEADS + n + 1))
                            for k in range(4):
                                ins = nc.tensor.matmul(banks[:, 4 * half + k, :], q_next[rows, g, t * P:(t + 1) * P],
                                                       keys[rows, g, k * CHUNK:(k + 1) * CHUNK], start=True, stop=True)
                            ins.then_inc(max_filled, 1)
                    pe.wait_ge(max_filled, c * (TILES * HEADS) + TILES * HEADS)
                    pe.sem_inc(max_chunk_used, 1)
                pe.wait_ge(max_taken, CHUNKS * TILES * HEADS + 2)

            def scores(c, j):
                group, k = j // 2 // KEY_TILES, j // 2 % KEY_TILES
                g = 2 * (group % GROUPS) + j % 2
                if k == 0 and j % 2 == 0:
                    pe.wait_ge(q_ready, GROUPS * c + (group + 1))
                    if isinstance(c, int) and group == 1:
                        pe.wait_ge(other_keys_loaded[0], LOADS)
                        pe.wait_ge(other_keys_loaded[1], LOADS)
                if isinstance(c, int) and 3 <= j < HALVES:
                    pe.wait_ge(exp_done, j - 2)
                elif j >= 2 and (j >= HALVES or not isinstance(c, int)):
                    pe.wait_ge(exp_done, HALVES * c + (j - 1))
                for half in range(2):
                    rows = slice(half * HALF, half * HALF + ROWS)
                    ins = nc.tensor.matmul(banks[:, score_bank(c, j) + half, :], keys[rows, g, k * P:(k + 1) * P],
                                           q_now[rows, g, :], start=True, stop=True)
                ins.then_inc(scores_ready, 1)

            def weigh_values(c, u):
                group, k = u // KEY_TILES, u % KEY_TILES
                pe.wait_ge(exp_done, HALVES * c + 2 * (u + 1))
                if isinstance(c, int) and u == 0:
                    pe.wait_ge(values_ready, 3)
                if isinstance(c, int) and u == 12:
                    pe.wait_ge(values_ready, 4)
                if k == 0 and (group > 0 or not isinstance(c, int)):
                    pe.wait_ge(acc_taken, GROUPS * c + group)
                for strip in range(4):
                    half, side = strip // 2, strip % 2
                    head = 2 * group + side + PAIRS * half
                    ins = nc.tensor.matmul(banks[32 * strip:32 * strip + 32, ACC, :],
                                           values[:, k, head * VW:head * VW + 32],
                                           probs[:, u % 2, side, half * CHUNK:(half + 1) * CHUNK],
                                           start=(k == 0), stop=(k == KEY_TILES - 1), tile_position=(0, 32 * strip))
                ins.then_inc(pv_done, 1)

            def transpose4(bank, src_of_tile, rows=P):
                for t in range(TILES):
                    ins = nc.tensor.transpose(banks[0:rows, bank, t * P:(t + 1) * P], src_of_tile(t), ident[:])
                return ins

            def untranspose_group(c, group, filled):
                pe.wait_ge(acc_taken, GROUPS * c + (group + 1))
                transpose4(Y if isinstance(c, int) and filled is attn_filled else W0,
                           lambda t: heads_raw[:, group, t * P:(t + 1) * P]).then_inc(filled, 1)

            def ffn_job(f, job, tail=False):
                freed = FFN_JOBS * (f + 1)
                if job == J_LAST_GROUP:
                    pe.wait_ge(ffn_freed, freed)
                    pe.wait_ge(attn_freed, ATTN_JOBS * (f + 1))
                    untranspose_group(f, GROUPS - 1, ffn_filled)
                elif job == J_ATTN_T:
                    pe.wait_ge(ffn_freed, freed + (J_LAST_GROUP + 1))
                    transpose4(W1, lambda t: attn[:, t, :]).then_inc(ffn_filled, 1)
                elif job == J_PROJ:
                    pe.wait_ge(ffn_freed, freed + (J_ATTN_T + 1))
                    for t in range(TILES):
                        ins = nc.tensor.matmul(banks[:, W0, t * P:(t + 1) * P], attnT[:, t * P:(t + 1) * P], wo_sb[:],
                                               start=True, stop=True)
                    ins.then_inc(ffn_filled, 1)
                elif job == J_X1T:
                    for t in range(TILES):
                        pe.wait_ge(x1_ready, TILES * f + (t + 1))
                        ins = nc.tensor.transpose(banks[:, W1, t * P:(t + 1) * P], x1[:, t, :], ident[:])
                    ins.then_inc(ffn_filled, 1)
                elif job == J_ROUTER:
                    pe.wait_ge(ffn_freed, freed + (J_X1T + 1))
                    for t in range(TILES):
                        ins = nc.tensor.matmul(banks[:, W0, t * EXPERTS:(t + 1) * EXPERTS], x1T[:, t * P:(t + 1) * P],
                                               router_sb[:], start=True, stop=True)
                    ins.then_inc(ffn_filled, 1)
                elif job == J_PROBS_T:
                    pe.wait_ge(weights_chosen, f + 1)
                    transpose4(ACC if tail else W1, lambda t: route[:, 7, t, :], rows=EXPERTS).then_inc(ffn_filled, 1)
                elif job == J_Y:
                    pe.wait_ge(y_taken, f + 2)
                    pe.wait_ge(ffn_freed, freed + J_Y)
                    transpose4(W0, lambda t: yT[:, t * P:(t + 1) * P]).then_inc(ffn_filled, 1)

            def gate(f, s, tail):
                bank = TAIL_BANKS[s % 3] if tail else W0
                last = J_SLICE0 + s - 1 if not tail else J_X1T if s < 2 else J_ROUTER if s == 2 else J_SLICE0 + s - 3
                pe.wait_ge(ffn_freed, FFN_JOBS * (f + 1) + (tail_place(last) if tail else last + 1))
                if s == 0:
                    pe.wait_ge(weights_loaded, 48)
                nc.tensor.matmul(banks[:, bank, :], gate_sb[:, s * P:(s + 1) * P], x1T[:], start=True, stop=True) \
                    .then_inc(gate_filled, 1)

            def up(f, s, tail):
                bank = TAIL_BANKS[s % 3] if tail else W0
                nc.tensor.matmul(banks[:, bank + 1, :], up_sb[:, s * P:(s + 1) * P], x1T[:], start=True, stop=True) \
                    .then_inc(ffn_filled, 1)

            def down(f, s, tail=False):
                if s == 0:
                    pe.wait_ge(y_taken, f + 1)
                if tail:
                    pe.wait_ge(tail_weighted_ready, s + 1)
                else:
                    pe.wait_ge(ffn_freed, FFN_JOBS * (f + 1) + (J_SLICE0 + s + 1))
                nc.tensor.matmul(banks[:, Y, :], down_sb[:, s, :],
                                 tail_hidden[:, s % TAIL_BUFFERS, :] if tail else weighted[:, s % 4, :],
                                 start=(s == 0), stop=False).then_inc(down_done, 1)
                if s == SLICES - 1:
                    nc.tensor.matmul(banks[:, Y, :], down_bias[:], routeT[:], start=False, stop=True) \
                        .then_inc(y_filled, 1)

            def attention(c, with_ffn):
                for u in range(UNITS):
                    if isinstance(c, int):
                        for j in (2 * u + 3, 2 * u + 4):
                            if j < HALVES:
                                scores(c, j)
                        if u == UNITS - 1:
                            scores(c, HALVES)
                            scores(c, HALVES + 1)
                    else:
                        scores(c, 2 * u + 2)
                        if u % KEY_TILES == 1 and u > KEY_TILES:
                            pe.wait_ge(ffn_freed, FFN_JOBS * c + (J_SLICE0 + sum(a < u for a in UP_AT)))
                            untranspose_group(c, u // KEY_TILES - 1, attn_filled)
                        ffn_work(c - 1, u)
                        scores(c, 2 * u + 3)
                    weigh_values(c, u)
                    if not with_ffn and u % KEY_TILES == 1 and u > KEY_TILES:
                        if u > 2 * KEY_TILES:
                            pe.wait_ge(attn_freed, u // KEY_TILES - 1)
                        else:
                            pe.wait_ge(consts_loaded, CONSTS_LOADED)
                            pe.wait_ge(values_ready, 4)
                        untranspose_group(c, u // KEY_TILES - 1, attn_filled)

            def ffn_work(f, u):
                if u in JOB_AT:
                    ffn_job(f, JOB_AT[u])
                if u in GATE_AT:
                    group = (u - 2) // KEY_TILES
                    if group:
                        pe.wait_ge(attn_freed, ATTN_JOBS * (f + 1) + group)
                    gate(f, GATE_AT.index(u), False)
                if u in UP_AT:
                    up(f, UP_AT.index(u), False)
                if u in DOWN_AT:
                    down(f, DOWN_AT.index(u))
                if u == Y_AT:
                    ffn_job(f, J_Y)

            for k in range(KEY_TILES):
                ins = nc.tensor.matmul(banks[:, V_BANKS[k // 4], k % 4 * P:(k % 4 + 1) * P],
                                       xT_sb[:, k * P:(k + 1) * P], wqkv_sb[:, 2 * HID:3 * HID], start=True, stop=True)
                if k % 4 == 3:
                    ins.then_inc(v_filled, 1)
            for half in range(2):
                pe.wait_ge(keys_loaded[half], KEYS_LOADED)
            scores(0, 0)
            scores(0, 1)
            pe.wait_ge(values_ready, 2)
            scores(0, 2)
            attention(0, False)
            with pe.Fori(1, CHUNKS) as c:
                attention(c, True)
            f = CHUNKS - 1
            for job in range(J_PROBS_T):
                ffn_job(f, job)
            for s in range(SLICES + TAIL_LAG):
                if s == TAIL_FIRST:
                    ffn_job(f, J_PROBS_T, True)
                if s < SLICES:
                    gate(f, s, True)
                    up(f, s, True)
                if s >= TAIL_LAG:
                    down(f, s - TAIL_LAG, True)
            ffn_job(f, J_Y)


def kernel(**inputs):
    import numpy as _np
    import concourse.bacc as _bacc
    from concourse.bass_utils import run_bass_kernel_spmd as _run

    a = {k: _np.asarray(v) for k, v in inputs.items()}
    x = a["L0_attn_x"].reshape(TOKENS, HID)
    by_head = _np.arange(HID).reshape(HEADS, D)
    order = _np.concatenate([by_head.T.reshape(-1), HID + by_head.T.reshape(-1), 2 * HID + _np.arange(HID)])
    arrays = {
        "x": x,
        "xT": x.T,
        "wqkvT": a["L0_attn_w_qkv"][order].T,
        "woT": a["L0_attn_w_o"].T,
        "routerT": a["L0_ffn_router_w"].T,
        "gate_w": a["L0_ffn_gate_w"],
        "gate_b": a["L0_ffn_gate_b"].reshape(SLICES, P).T,
        "up_w": a["L0_ffn_up_w"],
        "up_b": a["L0_ffn_up_b"].reshape(SLICES, P).T,
        "down_w": a["L0_ffn_down_w"],
        "down_b": a["L0_ffn_down_b"],
        "identity": _np.eye(P, dtype=_np.float32),
        "head_of": _np.tile(_np.eye(HEADS, 32, dtype=_np.float32), (D, 1)),
        "rank": _np.tile(_np.arange(EXPERTS, 0, -1, dtype=_np.float32), (P, TILES, 1)),
    }
    arrays = {f"in_{k}": _np.ascontiguousarray(v) for k, v in arrays.items()}
    nc = _bacc.Bacc("TRN2", target_bir_lowering=False, num_devices=1)
    args = [nc.dram_tensor(k, v.shape, mybir.dt.from_np(v.dtype), kind="ExternalInput").ap() for k, v in arrays.items()]
    out = nc.dram_tensor("out", (TOKENS, HID), F32, kind="ExternalOutput").ap()
    build_layer(nc, *args, out)
    r = _run(nc, [arrays], core_ids=[0])
    return r.results[0]["out"].reshape(1, TOKENS, HID)
```
